# Optimizing a Trainium2 kernel written in Bass

```python
import numpy as np
import jax
import jax.numpy as jnp

def _softmax(x, axis=-1):
    return jax.nn.softmax(x, axis=axis)

def _gelu(x):
    return jax.nn.gelu(x, approximate=True)

def _silu(x):
    return jax.nn.silu(x)

def _sigmoid(x):
    return jax.nn.sigmoid(x)

def _layernorm(x, axis=-1, eps=1e-05):
    m = jnp.mean(x, axis=axis, keepdims=True)
    v = jnp.var(x, axis=axis, keepdims=True)
    return (x - m) / jnp.sqrt(v + eps)

def _scatter_add(tgt, idx, src, axis=0):
    return tgt.at[idx].add(src)

def _segment_sum(src, seg, n):
    return jax.ops.segment_sum(src, seg, n)
kernel_name = 'mk_flamingo_gated_d1_seqx_r4_27bb30'

def setup_inputs(seed: int=0):
    np.random.seed(seed)
    _w = jnp.asarray

    def _rec_inputs():
        import jax
        import jax.numpy as jnp
        _rk = jax.random.key(seed)
        x = 7.22e-05 + 1 * jax.random.normal(jax.random.fold_in(_rk, 1), (16, 256, 256), jnp.float32)
        _lenS = 256 - jax.random.randint(jax.random.fold_in(_rk, 7), (16,), 0, max(1, 256 // 4) + 1, jnp.int32)
        _lenS2 = 256 - jax.random.randint(jax.random.fold_in(_rk, 8), (16,), 0, max(1, 256 // 4) + 1, jnp.int32)
        _ctx_1024P = jax.random.normal(jax.random.fold_in(_rk, 11), (16, 16, 256), jnp.float32)
        _ctx_1024c = jax.random.dirichlet(jax.random.fold_in(_rk, 511), 0.3 * jnp.ones((16,), jnp.float32), (16, 256))
        _ctx_1024t = jnp.einsum('bsk,bkd->bsd', _ctx_1024c, _ctx_1024P)
        _ctx_1024t = _ctx_1024t * jax.lax.rsqrt(jnp.mean(jnp.square(_ctx_1024t)) + 1e-12) * 0.953939
        ctx_1024 = 4.13588e-05 + 0.999923 * (_ctx_1024t + 0.3 * jax.random.normal(jax.random.fold_in(_rk, 611), (16, 256, 256), jnp.float32))
        _g = jax.random.normal(jax.random.fold_in(_rk, 9001), (2, 1), jnp.float32)
        _g = jnp.sign(_g) * jnp.maximum(jnp.abs(_g), 1.0) + (_g == 0) * 1.0
        g_xattn = _g[0]
        g_ffn = _g[1]
        return (x, ctx_1024, g_xattn, g_ffn)
    x, ctx_1024, g_xattn, g_ffn = _rec_inputs()

    def _L0_xattn_setup():
        import jax, jax.numpy as jnp
        import numpy as np
        import math
        BSZ, SEQ, DIM, NHEADS = (4, 512, 256, 16)
        HEAD_DIM = DIM // NHEADS
        key = jax.random.key(seed)
        ks = jax.random.split(key, 7)
        s = 1.0 / math.sqrt(DIM)
        return {'q': jax.random.normal(ks[0], (BSZ, SEQ, DIM), jnp.float32), 'k': jax.random.normal(ks[1], (BSZ, SEQ, DIM), jnp.float32), 'v': jax.random.normal(ks[2], (BSZ, SEQ, DIM), jnp.float32), 'wq': jax.random.normal(ks[3], (DIM, DIM), jnp.float32) * s, 'wk': jax.random.normal(ks[4], (DIM, DIM), jnp.float32) * s, 'wv': jax.random.normal(ks[5], (DIM, DIM), jnp.float32) * s, 'wo': jax.random.normal(ks[6], (DIM, DIM), jnp.float32) * s}
    _L0_xattn_all = _L0_xattn_setup()
    _L0_xattn_in = {k: v for k, v in _L0_xattn_all.items() if k in ('wq', 'wk', 'wv', 'wo')}
    del _L0_xattn_all

    def _L0_ffn_setup():
        import jax, jax.numpy as jnp
        import numpy as np
        B, S, D_MODEL, D_FF, E, R, TOP_K = (4, 512, 256, 1024, 8, 16, 2)
        key = jax.random.key(seed)
        ks = jax.random.split(key, 9)
        sd = 1.0 / np.sqrt(D_MODEL)
        return {'hidden_states': jax.random.normal(ks[0], (B, S, D_MODEL), jnp.float32), 'wi': jax.random.normal(ks[1], (D_FF, D_MODEL), jnp.float32) * sd, 'bi': jax.random.normal(ks[2], (D_FF,), jnp.float32) * 0.01, 'wo': jax.random.normal(ks[3], (D_MODEL, D_FF), jnp.float32) * (1.0 / np.sqrt(D_FF)), 'bo': jax.random.normal(ks[4], (D_MODEL,), jnp.float32) * 0.01, 'lora_A': jax.random.normal(ks[5], (E, R, D_MODEL), jnp.float32) * sd, 'lora_B': jax.random.normal(ks[6], (E, D_FF, R), jnp.float32) * 0.02, 'gate_w': jax.random.normal(ks[7], (E, D_MODEL), jnp.float32) * sd, 'gate_b': jax.random.normal(ks[8], (E,), jnp.float32) * 0.01}
    _L0_ffn_all = _L0_ffn_setup()
    _L0_ffn_in = {k: v for k, v in _L0_ffn_all.items() if k in ('wi', 'bi', 'wo', 'bo', 'lora_A', 'lora_B', 'gate_w', 'gate_b')}
    del _L0_ffn_all
    return {'x': x, 'ctx_1024': ctx_1024, 'g_xattn': g_xattn, 'g_ffn': g_ffn, 'L0_xattn_wq': _L0_xattn_in['wq'], 'L0_xattn_wk': _L0_xattn_in['wk'], 'L0_xattn_wv': _L0_xattn_in['wv'], 'L0_xattn_wo': _L0_xattn_in['wo'], 'L0_ffn_wi': _L0_ffn_in['wi'], 'L0_ffn_bi': _L0_ffn_in['bi'], 'L0_ffn_wo': _L0_ffn_in['wo'], 'L0_ffn_bo': _L0_ffn_in['bo'], 'L0_ffn_lora_A': _L0_ffn_in['lora_A'], 'L0_ffn_lora_B': _L0_ffn_in['lora_B'], 'L0_ffn_gate_w': _L0_ffn_in['gate_w'], 'L0_ffn_gate_b': _L0_ffn_in['gate_b']}

def reference(x, ctx_1024, g_xattn, g_ffn, L0_xattn_wq, L0_xattn_wk, L0_xattn_wv, L0_xattn_wo, L0_ffn_wi, L0_ffn_bi, L0_ffn_wo, L0_ffn_bo, L0_ffn_lora_A, L0_ffn_lora_B, L0_ffn_gate_w, L0_ffn_gate_b):
    import jax
    import jax.numpy as jnp

    def _L0_xattn_ref(q, k, v, wq, wk, wv, wo):
        import jax, jax.numpy as jnp
        import numpy as np
        import math
        BSZ, SEQ, DIM, NHEADS = (4, 512, 256, 16)
        HEAD_DIM = DIM // NHEADS
        bsz, seqlen, _ = q.shape
        xq = (q @ wq.T).reshape(bsz, seqlen, NHEADS, HEAD_DIM).transpose(0, 2, 1, 3)
        xk = (k @ wk.T).reshape(bsz, seqlen, NHEADS, HEAD_DIM).transpose(0, 2, 1, 3)
        xv = (v @ wv.T).reshape(bsz, seqlen, NHEADS, HEAD_DIM).transpose(0, 2, 1, 3)
        scores = jnp.einsum('bhqd,bhkd->bhqk', xq, xk) / math.sqrt(HEAD_DIM)
        causal = jnp.tril(jnp.ones((seqlen, seqlen), dtype=bool))
        scores = jnp.where(causal[None, None], scores, -jnp.inf)
        attn = jax.nn.softmax(scores.astype(jnp.float32), axis=-1).astype(xq.dtype)
        out = jnp.einsum('bhqk,bhkd->bhqd', attn, xv)
        out = out.transpose(0, 2, 1, 3).reshape(bsz, seqlen, NHEADS * HEAD_DIM)
        return out @ wo.T

    def _L0_ffn_ref(hidden_states, wi, bi, wo, bo, lora_A, lora_B, gate_w, gate_b):
        import jax, jax.numpy as jnp
        import numpy as np
        B, S, D_MODEL, D_FF, E, R, TOP_K = (4, 512, 256, 1024, 8, 16, 2)
        logits = jnp.einsum('bsd,ed->bse', hidden_states, gate_w) + gate_b
        scores = jax.nn.softmax(logits, axis=-1)
        top_v, top_i = jax.lax.top_k(scores, TOP_K)
        val_sum = top_v.sum(axis=-1)
        out = jnp.zeros_like(hidden_states)
        for e in range(E):
            count = (top_i == e).sum(axis=-1).astype(hidden_states.dtype)
            gate = count * val_sum
            inter = jnp.einsum('bsd,fd->bsf', hidden_states, wi) + bi + jnp.einsum('bsr,fr->bsf', jnp.einsum('bsd,rd->bsr', hidden_states, lora_A[e]), lora_B[e])
            h = jax.nn.relu(inter)
            expert_out = jnp.einsum('bsf,df->bsd', h, wo) + bo
            out = out + gate[..., None] * expert_out
        return out
    x = x + jnp.tanh(g_xattn[0]) * _L0_xattn_ref(_layernorm(x, axis=-1), ctx_1024, ctx_1024, L0_xattn_wq, L0_xattn_wk, L0_xattn_wv, L0_xattn_wo)
    x = x + jnp.tanh(g_ffn[0]) * _L0_ffn_ref(_layernorm(x, axis=-1), L0_ffn_wi, L0_ffn_bi, L0_ffn_wo, L0_ffn_bo, L0_ffn_lora_A, L0_ffn_lora_B, L0_ffn_gate_w, L0_ffn_gate_b)
    return x

_drawn_inputs = setup_inputs


def setup_inputs(seed=0):
    import zlib

    import numpy as np

    out = dict(_drawn_inputs(seed))
    spreads = {}
    factors = {'L0_ffn_bi': 8.0, 'L0_ffn_bo': 7.302, 'L0_ffn_gate_b': 8.0}
    for name, (base, spread) in spreads.items():
        noise = np.random.default_rng([zlib.crc32(name.encode()), seed]).standard_normal(out[name].shape)
        drawn = base * np.exp(spread * noise) if base else spread * noise
        out[name] = jnp.asarray(drawn.astype(out[name].dtype))
    for name, factor in factors.items():
        out[name] = (out[name] * factor).astype(out[name].dtype)
    return out
```

```python
from contextlib import ExitStack

import numpy as np
import concourse.bass as bass
from concourse import mybir

F32 = mybir.dt.float32
F32R = mybir.dt.float32r
BF16 = mybir.dt.bfloat16
I32 = mybir.dt.int32
ALU = mybir.AluOpType
ACT = mybir.ActivationFunctionType
AX = mybir.AxisListType

P = 128
BATCH, SEQ, D = 16, 256, 256
HEADS, HD = 16, 16
FF, EXPERTS, RANK = 1024, 8, 16
EPS = 1e-5
GB = 2
GT = GB * SEQ
GROUPS = BATCH // GB
TT = GT // P
DK = D // P
QUADS = HEADS // 4
HSLOT = 32
CHUNKS = FF // P
NAG = EXPERTS * RANK + EXPERTS
SPLITS = 3
SROWS = SPLITS * HD
HALF = 8
SCALE = 1.0 / float(np.sqrt(HD))
MASKED = -1e30
RSQRT_MAGIC = 0x5F3759DF


def plan(fills):
    count, where = {}, {}
    for name, bank in fills:
        where[name] = (bank, count.get(bank, 0))
        count[bank] = count.get(bank, 0) + 1
    return where, count


FRONT = [("xT", 0), ("xT", 1), ("q", 0), ("q", 1), ("k", 0), ("k", 1), ("v", 0), ("v", 1)]
SCORES = []
for _b in range(GB):
    SCORES += [("S", _b, _q, _p) for _q in range(QUADS) for _p in range(3)] + [("mT", _b)]
PROBS = []
for _u in range(GB * QUADS + 1):
    if _u < GB * QUADS:
        PROBS += [("ST", _u // QUADS, _u % QUADS, _p) for _p in range(3)]
    if _u > 0:
        _v = _u - 1
        PROBS += [("AV", _v // QUADS, _v % QUADS)]
        if _v % 2:
            PROBS += [("norm", _v // QUADS, (_v % QUADS) // 2)]
FFN = []
for _c in range(CHUNKS + 3):
    if _c < CHUNKS:
        FFN.append(("up1", _c))
    if 0 <= _c - 1 < CHUNKS:
        FFN.append(("up2", _c - 1))
    if 0 <= _c - 2 < CHUNKS:
        FFN.append(("split", _c - 2))
    if 0 <= _c - 3 < CHUNKS:
        FFN.append(("down", _c - 3))
FFN += [("out", 0), ("out", 1)]
MID = [("wo", 0), ("wo", 1), ("ln2",), ("x2T", 0), ("x2T", 1), ("ag", 0), ("ag", 1), ("route",), ("aT", 0), ("aT", 1)]

_rot = [s for s in FRONT + SCORES + PROBS if s[0] not in ("AV", "norm")]
A_FILLS, A_COUNT = plan([(s, n % 3) for n, s in enumerate(_rot)]
                        + [(("AV", b, pair), 3) for b in range(GB) for pair in range(QUADS // 2)])
M_FILLS, M_COUNT = plan([(("wo", 0), 4), (("wo", 1), 5), (("x2T", 0), 6), (("x2T", 1), 7), (("ag", 0), 4),
                         (("ag", 1), 5), (("aT", 0), 6), (("aT", 1), 7)]
                        + [f for c in range(CHUNKS) for f in ((("up1", c), 4 + c % 2), (("up2", c), 4 + c % 2))]
                        + [(("down", 0), 6), (("down", 1), 7)])


def merge(a, b):
    out, i, j = [], 0, 0
    while i < len(a) or j < len(b):
        if j >= len(b) or (i < len(a) and i * len(b) <= j * len(a)):
            out.append(a[i])
            i += 1
        else:
            out.append(b[j])
            j += 1
    return out


EARLY = 6
ATTENTION = [("ln1",), ("xres",)] + FRONT[:2] + [("cx",)] + FRONT[2:] + SCORES + PROBS
FRONT_BOTH = [("ln1",), ("xT", 0), ("xT", 1), ("cx",), ("wo", 0), ("q", 0), ("wo", 1), ("xres",), ("q", 1), ("ln2",),
              ("k", 0), ("k", 1), ("x2T", 0), ("x2T", 1), ("v", 0), ("v", 1), ("ag", 0), ("ag", 1), ("route",)]
BOTH = (FRONT_BOTH + SCORES[:EARLY] + [("aT", 0), ("aT", 1)]
        + merge(SCORES[EARLY:] + PROBS, FFN))
LAST = MID + FFN
M_KINDS = {s[0] for s in MID + FFN}

NEWTON = 3
LN_LINKS = 5 + 4 * NEWTON
ROUTE_LINKS = 17
A_LINKS = LN_LINKS + 2 * 4
M_LINKS = LN_LINKS + ROUTE_LINKS
STACK_DMAS = SPLITS * HALF * 2


class Chain:

    def __init__(self, eng, sem, per):
        self.eng, self.sem, self.per, self.n, self.group = eng, sem, per, 0, 0

    def start(self, group):
        self.group, self.n = group, 0

    def link(self, ins):
        self.n += 1
        ins.then_inc(self.sem, 1)
        self.eng.wait_ge(self.sem, self.group * self.per + self.n)


def flamingo_layer(nc, x, ctxT, g_xattn, g_ffn, wqT, wkT, wvT, woT, wiT, bi, w2T, bo, abT, bT, gate_b, out):
    with ExitStack() as ctx:
        def sb(name, shape, dt):
            return ctx.enter_context(nc.sbuf_tensor(name, shape, dt))

        def sem(name):
            return ctx.enter_context(nc.semaphore(name))

        bank = [ctx.enter_context(nc.psum_tensor(f"bank{i}", [P, 512], F32)) for i in range(8)]

        def pair(name, n, cols):
            return sb(name + "_hi", [P, n, cols], F32R), sb(name + "_lo", [P, n, cols], F32R)

        wq, wk, wv = pair("wq", DK, D), pair("wk", DK, D), pair("wv", DK, D)
        wo = pair("wo", QUADS, D)
        ab = pair("ab", DK, NAG)
        wb = pair("wb", 1, FF)
        wi = pair("wi", DK, FF)
        w2 = pair("w2", CHUNKS, D)
        bi_sb = sb("bi_sb", [P, CHUNKS], F32)
        bo2 = sb("bo2", [P, D], F32)
        gb_sb = sb("gb_sb", [P, EXPERTS], F32)
        rank_sb = sb("rank_sb", [P, EXPERTS], F32)
        gates = sb("gates", [P, 2], F32)
        tanh_g = sb("tanh_g", [P, 2], F32)
        ident = sb("ident", [P, P], F32)
        ident_b = sb("ident_b", [P, P], BF16)
        causal = sb("causal", [P, 4, P], BF16)

        xin = sb("xin", [P, TT, D], F32)
        xres = sb("xres", [P, TT, D], F32)
        cin = sb("cin", [P, DK, GT], F32)
        c_hi, c_lo = pair("c", DK, GT)
        xn = sb("xn", [P, TT, D], F32)
        xT_hi, xT_lo = pair("xT", DK, GT)
        scratch = sb("scratch", [P, 4096], F32)
        compact = scratch[:, :].bitcast(F32R).rearrange("p (o m t) -> p o m t", o=4, m=DK)
        q_hi, q_lo, k_hi, k_lo = (compact[:, i] for i in range(4))
        probs = scratch[:, 0:3072].rearrange("p (s a t) -> p s a t", s=2, a=3)
        q_stack = sb("q_stack", [P, HALF, GT], F32R)
        k_stack = sb("k_stack", [P, HALF, GT], F32R)
        v_ones = sb("v_ones", [P, TT, HEADS, HSLOT], F32)
        neg_max = sb("neg_max", [P, GB, 2, HEADS], F32)
        max_row = sb("max_row", [2 * HEADS, GB, P], F32R)
        denom = sb("denom", [P, 512], F32)
        att = sb("att", [P, 2, SEQ], F32)
        att_hi, att_lo = pair("att", QUADS, GT)

        work = sb("work", [P, 5120], F32)
        x1 = work[:, 0:1024].rearrange("p (t d) -> p t d", t=TT)
        fin = work[:, 1024:2048].rearrange("p (t d) -> p t d", t=TT)
        a_all = work[:, 2048:2560].rearrange("p (t e) -> p t e", t=TT)
        a_first = work[:, 2560:3072].rearrange("p (t e) -> p t e", t=TT)
        a_diff = work[:, 3072:3584].rearrange("p (t e) -> p t e", t=TT)
        relu1 = work[:, 3584:4608].rearrange("p (s t) -> p s t", s=2)
        relu2 = work[:, 4608:5120]
        relu_sum = work[:, 2048:3072].rearrange("p (s t) -> p s t", s=2)
        a1_hi, a1_lo = pair("a1", 1, GT)
        a2_hi, a2_lo = pair("a2", 1, GT)
        h_hi, h_lo = c_hi, c_lo
        stats = sb("stats", [P, TT, 6], F32)
        moments = sb("moments", [P, TT, 2], F32)
        nt = sb("nt", [P, 3, TT], F32)
        lg = sb("lg", [P, TT, EXPERTS], F32)
        pr = sb("pr", [P, TT, EXPERTS], F32)
        pr2 = sb("pr2", [P, TT, EXPERTS], F32)
        key = sb("key", [P, TT, EXPERTS], F32)
        one1 = sb("one1", [P, TT, EXPERTS], F32)
        one2 = sb("one2", [P, TT, EXPERTS], F32)
        tk = sb("tk", [P, 8, TT], F32)
        gate_val = sb("gate_val", [P, TT], F32)

        full = [sem(f"full{i}") for i in range(8)]
        taken = [sem(f"taken{i}") for i in range(8)]
        w_loaded = sem("w_loaded")
        small_loaded = sem("small_loaded")
        w2_loaded = sem("w2_loaded")
        w_hi = sem("w_hi")
        w_lo = sem("w_lo")
        consts = sem("consts")
        pool_step = sem("pool_step")
        tanh_ready = sem("tanh_ready")
        x_loaded = sem("x_loaded")
        c_loaded = sem("c_loaded")
        c_hi_ready = sem("c_hi_ready")
        c_lo_ready = sem("c_lo_ready")
        xn1_ready = sem("xn1_ready")
        xres_ready = sem("xres_ready")
        hi_a = sem("hi_a")
        hi_m = sem("hi_m")
        q_stacked = sem("q_stacked")
        k_stacked = sem("k_stacked")
        max_stacked = [sem(f"max_stacked{b}") for b in range(GB)]
        masked = sem("masked")
        av_done = sem("av_done")
        att_hi_ready = sem("att_hi_ready")
        att_ready = sem("att_ready")
        xn2_ready = sem("xn2_ready")
        logits_shifted = sem("logits_shifted")
        exp_ready = sem("exp_ready")
        routed = sem("routed")
        sum_ready = sem("sum_ready")
        h_hi_ready = sem("h_hi_ready")
        h_ready = sem("h_ready")
        down_done = sem("down_done")
        out_ready = sem("out_ready")
        out_stored = sem("out_stored")
        dve_a = sem("dve_a")
        dve_m = sem("dve_m")
        dve_setup = sem("dve_setup")
        held = sem("held")

        def fill(step):
            where, count = (M_FILLS, M_COUNT) if step[0] in M_KINDS else (A_FILLS, A_COUNT)
            b, n = where[step]
            return b, n, count[b]

        def wait_full(eng, step, g):
            b, n, per = fill(step)
            eng.wait_ge(full[b], g * per + n + 1)

        def wait_taken(eng, step, g):
            b, n, per = fill(step)
            eng.wait_ge(taken[b], g * per + n + 1)

        def wait_free(eng, step, g, first):
            b, n, per = fill(step)
            if not first or n > 0:
                eng.wait_ge(taken[b], g * per + n)

        def wait_earlier(eng, s, g, per, n, first):
            if not first or n > 0:
                eng.wait_ge(s, g * per + n)

        def hold(eng):
            eng.sem_inc(held, 1)

        first_weights = []
        at = 0
        for dram, dst in ((wqT, wq), (wkT, wk), (wvT, wv), (woT, wo), (abT, ab), (bT, wb)):
            n, cols = dst[0].shape[1], dst[0].shape[2]
            first_weights.append((dram.rearrange("(n p) c -> p n c", p=P), dst,
                                  scratch[:, at:at + n * cols].rearrange("p (n c) -> p n c", n=n)))
            at += n * cols
        late_weights = []
        at = 0
        for dram, dst in ((wiT, wi), (w2T, w2)):
            n, cols = dst[0].shape[1], dst[0].shape[2]
            late_weights.append((dram.rearrange("(n p) c -> p n c", p=P), dst,
                                 work[:, at:at + n * cols].rearrange("p (n c) -> p n c", n=n)))
            at += n * cols
        NW = len(first_weights)
        NSMALL = 5

        x_rows = x.rearrange("(g t p) d -> g p t d", p=P, t=TT)
        out_rows = out.rearrange("(g t p) d -> g p t d", p=P, t=TT)
        c_cols = ctxT.rearrange("(n p) (g t) -> g p n t", p=P, g=GROUPS)

        block = ctx.enter_context(nc.Block())

        @block.sync
        def _(sp):
            def load_group(g, first):
                if not first:
                    sp.wait_ge(c_lo_ready, g)
                    sp.wait_ge(xres_ready, g)
                    sp.wait_ge(xn1_ready, g)
                sp.dma_start(xin[:], x_rows[g]).then_inc(x_loaded, 16)
                sp.dma_start(cin[:], c_cols[g]).then_inc(c_loaded, 16)

            def stack(g, m, pieces, dst, s):
                for i, src in enumerate(pieces):
                    for h in range(HALF):
                        sp.dma_start(dst[64 * m + HD * i:64 * m + HD * (i + 1), h, :].bitcast(F32),
                                     src[HD * h:HD * (h + 1), m, :].bitcast(F32)).then_inc(s, 16)

            def stack_max(g, b):
                wait_taken(sp, ("mT", b), g)
                for qt in range(2):
                    for m in range(2):
                        r = qt * HEADS + m * HALF
                        sp.dma_start(q_stack[64 * m + SROWS:64 * m + SROWS + 1, :,
                                             b * SEQ + qt * P:b * SEQ + (qt + 1) * P].bitcast(F32),
                                     max_row[r:r + HALF, b, :].bitcast(F32)).then_inc(max_stacked[b], 16)

            def store(f):
                for p in range(2):
                    sp.wait_ge(out_ready, f * 2 + p + 1)
                    sp.dma_start(out_rows[f][:, 2 * p:2 * p + 2, :], fin[:, 2 * p:2 * p + 2, :]).then_inc(out_stored, 16)

            def group(g, load_next=True, store_last=True):
                for m in range(DK):
                    wait_taken(sp, ("q", m), g)
                    stack(g, m, (q_hi, q_hi, q_lo), q_stack, q_stacked)
                for m in range(DK):
                    wait_taken(sp, ("k", m), g)
                    stack(g, m, (k_hi, k_lo, k_hi), k_stack, k_stacked)
                if load_next:
                    load_group(g + 1, False)
                for b in range(GB):
                    stack_max(g, b)
                if store_last:
                    store(g - 1)

            load_group(0, True)
            for src, _, stage in first_weights:
                sp.dma_start(stage, src).then_inc(w_loaded, 16)
            sp.dma_start(gates[:, 0:1], g_xattn.rearrange("(a b) -> a b", a=1).partition_broadcast(P)).then_inc(small_loaded, 16)
            sp.dma_start(gates[:, 1:2], g_ffn.rearrange("(a b) -> a b", a=1).partition_broadcast(P)).then_inc(small_loaded, 16)
            sp.dma_start(bi_sb[:], bi).then_inc(small_loaded, 16)
            sp.dma_start(bo2[:], bo.rearrange("(a b) -> a b", a=1).partition_broadcast(P)).then_inc(small_loaded, 16)
            sp.dma_start(gb_sb[:], gate_b.rearrange("(a b) -> a b", a=1).partition_broadcast(P)).then_inc(small_loaded, 16)
            for src, _, stage in late_weights:
                sp.dma_start(stage, src).then_inc(w2_loaded, 16)
            sp.wait_ge(consts, 1)
            group(0, store_last=False)
            with sp.Fori(1, GROUPS - 1) as g:
                group(g)
            group(GROUPS - 1, load_next=False)
            store(GROUPS - 1)
            sp.wait_ge(out_stored, 32 * GROUPS)

        @block.tensor
        def _(pe):
            def mm(*a, **k):
                return nc.tensor.matmul(*a, **k)

            def products(dst, lhs, rhs, tiles, more=False):
                todo = [(i, a, b) for i in range(tiles) for a, b in ((0, 0), (0, 1), (1, 0))]
                for n, (i, a, b) in enumerate(todo):
                    last = mm(dst, lhs[a](i), rhs[b](i), start=(n == 0 and not more), stop=(n == len(todo) - 1),
                              skip_group_check=more)
                return last

            def cols(pair_, lo, n):
                return [lambda i, t=t: t[:, i, lo:lo + n] for t in pair_]

            def step(s, g, f, first, first_f):
                kind = s[0]
                if kind in ("cx", "ln1", "ln2", "xres", "route", "split", "norm", "out"):
                    return
                if kind not in ("AV", "down"):
                    wait_free(pe, s, f if kind in M_KINDS else g, first_f if kind in M_KINDS else first)
                    ps = bank[fill(s)[0]]
                if kind == "xT":
                    if s[1] == 0:
                        pe.wait_ge(xn1_ready, g + 1)
                    for t in range(TT):
                        last = nc.tensor.transpose(ps[:, t * P:(t + 1) * P], xn[:, t, s[1] * P:(s[1] + 1) * P], ident[:])
                elif kind == "q":
                    if s[1] == 0:
                        wait_taken(pe, ("xT", 0), g)
                        wait_taken(pe, ("xT", 1), g)
                    last = products(ps[:], cols(wq, s[1] * P, P), cols((xT_hi, xT_lo), 0, GT), DK)
                elif kind == "k":
                    if s[1] == 0:
                        pe.wait_ge(c_hi_ready, g + 1)
                        pe.wait_ge(c_lo_ready, g + 1)
                    last = products(ps[:], cols(wk, s[1] * P, P), cols((c_hi, c_lo), 0, GT), DK)
                elif kind == "v":
                    for i in range(2):
                        last = products(ps[:, i * D:(i + 1) * D], cols((c_hi, c_lo), (2 * s[1] + i) * P, P), cols(wv, 0, D), DK)
                elif kind == "S":
                    _, b, quad, part = s
                    if (b, quad, part) == (0, 0, 0):
                        pe.wait_ge(q_stacked, (g + 1) * 16 * STACK_DMAS)
                        pe.wait_ge(k_stacked, (g + 1) * 16 * STACK_DMAS)
                    rows = slice(64 * (quad // 2), 64 * (quad // 2) + SROWS)
                    heads = range(4) if part == 0 else range(2 * part - 2, 2 * part)
                    width = P if part == 0 else SEQ
                    q0 = b * SEQ + (0 if part == 0 else P)
                    for n, j in enumerate(heads):
                        h = 4 * (quad % 2) + j
                        mm(ps[:, n * width:(n + 1) * width], q_stack[rows, h, q0:q0 + P],
                           k_stack[rows, h, b * SEQ:b * SEQ + width], start=(n == 0), stop=False, skip_group_check=True)
                    edge = ps[:].rearrange("p (n w) -> p n w", w=width)[:, :, width - P:width]
                    last = mm(edge, ident_b[:], causal[:, 0:len(heads), :], start=False, stop=True, skip_group_check=True)
                elif kind == "mT":
                    wait_taken(pe, ("S", s[1], QUADS - 1, 2), g)
                    last = nc.tensor.transpose(ps[0:2 * HEADS, 0:P], neg_max[:, s[1]].rearrange("p a h -> p (a h)"), ident[:])
                elif kind == "ST":
                    _, b, quad, part = s
                    if (quad, part) == (0, 0):
                        pe.wait_ge(max_stacked[b], (g + 1) * 64)
                    rows = slice(64 * (quad // 2), 64 * (quad // 2) + SROWS + 1)
                    heads = range(4) if part == 2 else range(2 * part, 2 * part + 2)
                    width = P if part == 2 else SEQ
                    k0 = b * SEQ + (P if part == 2 else 0)
                    for n, j in enumerate(heads):
                        h = 4 * (quad % 2) + j
                        last = mm(ps[:, n * width:(n + 1) * width], k_stack[rows, h, k0:k0 + P],
                                  q_stack[rows, h, (b + 1) * SEQ - width:(b + 1) * SEQ], start=True, stop=True)
                elif kind == "AV":
                    _, b, quad = s
                    u = b * QUADS + quad
                    pe.wait_ge(masked, g * 3 * GB * QUADS + 3 * (u + 1))
                    ps = bank[3]
                    if quad % 2 == 0:
                        wait_free(pe, ("AV", b, quad // 2), g, first)
                    c0 = (quad % 2) * SEQ
                    for kt in range(2):
                        for j in range(4):
                            src = probs[:, u % 2, j // 2, (j % 2) * SEQ:(j % 2 + 1) * SEQ] if kt == 0 else \
                                probs[:, u % 2, 2, j * P:(j + 1) * P]
                            last = mm(ps[HSLOT * j:HSLOT * (j + 1), c0 + kt * P:c0 + SEQ],
                                      v_ones[:, 2 * b + kt, 4 * quad + j, :], src,
                                      start=(kt == 0), stop=(kt == 1), skip_group_check=True)
                    last.then_inc(full[3] if quad % 2 else av_done, 1)
                    return
                elif kind == "wo":
                    pe.wait_ge(att_ready, f * 4 + 2 * (s[1] + 1))
                    for i in range(2):
                        last = products(ps[:, i * D:(i + 1) * D], cols((att_hi, att_lo), (2 * s[1] + i) * P, P),
                                        cols(wo, 0, D), QUADS)
                elif kind == "x2T":
                    if s[1] == 0:
                        pe.wait_ge(xn2_ready, f + 1)
                    for t in range(TT):
                        last = nc.tensor.transpose(ps[:, t * P:(t + 1) * P], xn[:, t, s[1] * P:(s[1] + 1) * P], ident[:])
                elif kind == "ag":
                    if s[1] == 0:
                        wait_taken(pe, ("x2T", 0), f)
                        wait_taken(pe, ("x2T", 1), f)
                    for i in range(2):
                        last = products(ps[:, i * D:i * D + NAG], cols((xT_hi, xT_lo), (2 * s[1] + i) * P, P), cols(ab, 0, NAG), DK)
                elif kind == "aT":
                    if s[1] == 0:
                        pe.wait_ge(routed, f + 1)
                    src = (a_first, a_diff)[s[1]]
                    for t in range(TT):
                        last = nc.tensor.transpose(ps[:, t * P:(t + 1) * P], src[:, t, :], ident[:])
                elif kind == "up1":
                    c = s[1]
                    if c == 0:
                        wait_taken(pe, ("aT", 0), f)
                        wait_taken(pe, ("aT", 1), f)
                    products(ps[:], cols(wi, c * P, P), cols((xT_hi, xT_lo), 0, GT), DK)
                    last = products(ps[:], cols(wb, c * P, P), cols((a1_hi, a1_lo), 0, GT), 1, more=True)
                elif kind == "up2":
                    last = products(ps[:], cols(wb, s[1] * P, P), cols((a2_hi, a2_lo), 0, GT), 1, more=True)
                elif kind == "down":
                    c = s[1]
                    pe.wait_ge(h_ready, f * CHUNKS + c + 1)
                    for t in range(TT):
                        p = t // 2
                        if c == 0 and t % 2 == 0:
                            wait_free(pe, ("down", p), f, first_f)
                        dst = bank[6 + p][:, (t % 2) * D:(t % 2 + 1) * D]
                        for n, (a, b) in enumerate(((h_hi, 0), (h_hi, 1), (h_lo, 0))):
                            last = mm(dst, a[:, c % 2, t * P:(t + 1) * P], w2[b][:, c, :],
                                      start=(c == 0 and t % 2 == 0 and n == 0), stop=(c == CHUNKS - 1 and n == 2),
                                      skip_group_check=True)
                        if c == CHUNKS - 1 and t % 2:
                            last.then_inc(full[6 + p], 1)
                    if c < CHUNKS - 1:
                        last.then_inc(down_done, 1)
                    return
                last.then_inc(full[fill(s)[0]], 1)

            def steps(todo, g, first=False, first_f=False):
                for s in todo:
                    step(s, g, g - 1, first, first_f)

            pe.wait_ge(consts, 2)
            pe.wait_ge(w_lo, NW)
            steps(ATTENTION, 0, first=True)
            pe.wait_ge(w_lo, NW + len(late_weights))
            steps(BOTH, 1, first_f=True)
            with pe.Fori(2, GROUPS) as g:
                steps(BOTH, g)
            steps(LAST, GROUPS)

        @block.scalar
        def _(act):
            def copy(dst, src):
                return nc.scalar.activation(dst, src, ACT.Copy)

            def split_weights(weights, loaded):
                for n, (_, dst, stage) in enumerate(weights):
                    act.wait_ge(loaded, 16 * len(weights))
                    copy(dst[0][:], stage).then_inc(w_hi, 1)

            def step(s, g, f, first, first_f):
                kind = s[0]
                if kind == "cx":
                    act.wait_ge(c_loaded, 16 * (g + 1))
                    copy(c_hi[:], cin[:]).then_inc(c_hi_ready, 1)
                elif kind == "xT":
                    wait_full(act, s, g)
                    copy(xT_hi[:, s[1], :], bank[fill(s)[0]][:]).then_inc(hi_a, 1)
                elif kind in ("q", "k"):
                    wait_full(act, s, g)
                    copy((q_hi if kind == "q" else k_hi)[:, s[1], :], bank[fill(s)[0]][:]).then_inc(hi_a, 1)
                elif kind == "v":
                    wait_full(act, s, g)
                    b = fill(s)[0]
                    for i in range(2):
                        last = copy(v_ones[:, 2 * s[1] + i, :, 0:HD], bank[b][:, i * D:(i + 1) * D].rearrange("p (h d) -> p h d", h=HEADS))
                    last.then_inc(taken[b], 1)
                elif kind == "mT":
                    wait_full(act, s, g)
                    b = fill(s)[0]
                    copy(max_row[:, s[1], :], bank[b][0:2 * HEADS, 0:P]).then_inc(taken[b], 1)
                elif kind == "ST":
                    _, bt, quad, part = s
                    u = bt * QUADS + quad
                    b = fill(s)[0]
                    wait_full(act, s, g)
                    if part == 0:
                        wait_earlier(act, full[3] if quad % 2 else av_done, g, GB * QUADS // 2, u // 2, first)
                    nc.scalar.activation(probs[:, u % 2, part, :], bank[b][:], ACT.Exp, scale=SCALE).then_inc(taken[b], 1)
                elif kind == "norm":
                    _, b, pr_ = s
                    wait_taken(act, ("AV", b, pr_), g)
                    copy(att_hi[:, 2 * pr_:2 * pr_ + 2, b * SEQ:(b + 1) * SEQ], att[:]).then_inc(att_hi_ready, 1)
                elif kind == "x2T":
                    wait_full(act, s, f)
                    copy(xT_hi[:, s[1], :], bank[fill(s)[0]][:]).then_inc(hi_m, 1)
                elif kind == "ag":
                    wait_full(act, s, f)
                    copy(a_all[:, 2 * s[1]:2 * s[1] + 2, :],
                         bank[fill(s)[0]][:].rearrange("p (t c) -> p t c", t=2)[:, :, 0:P]).then_inc(hi_m, 1)
                elif kind == "route":
                    act.wait_ge(logits_shifted, f + 1)
                    nc.scalar.activation(pr[:], lg[:], ACT.Exp).then_inc(exp_ready, 1)
                elif kind == "aT":
                    wait_full(act, s, f)
                    copy((a1_hi, a2_hi)[s[1]][:, 0, :], bank[fill(s)[0]][:]).then_inc(hi_m, 1)
                elif kind == "up1":
                    c = s[1]
                    b = fill(s)[0]
                    wait_full(act, s, f)
                    wait_earlier(act, sum_ready, f, CHUNKS, c - 1, first_f)
                    nc.scalar.activation(relu1[:, c % 2, :], bank[b][:], ACT.Relu, bias=bi_sb[:, c:c + 1]).then_inc(taken[b], 1)
                elif kind == "up2":
                    c = s[1]
                    b = fill(s)[0]
                    wait_full(act, s, f)
                    wait_earlier(act, sum_ready, f, CHUNKS, c, first_f)
                    nc.scalar.activation(relu2, bank[b][:], ACT.Relu, bias=bi_sb[:, c:c + 1]).then_inc(taken[b], 1)
                elif kind == "split":
                    c = s[1]
                    act.wait_ge(sum_ready, f * CHUNKS + c + 1)
                    if c >= 2:
                        act.wait_ge(down_done, f * (CHUNKS - 1) + c - 1)
                    copy(h_hi[:, c % 2, :], relu_sum[:, c % 2, :]).then_inc(h_hi_ready, 1)

            def steps(todo, g, first=False, first_f=False):
                for s in todo:
                    step(s, g, g - 1, first, first_f)

            split_weights(first_weights, w_loaded)
            act.wait_ge(small_loaded, 16 * NSMALL)
            nc.scalar.activation(tanh_g[:], gates[:], ACT.Tanh).then_inc(tanh_ready, 1)
            steps(ATTENTION, 0, first=True)
            split_weights(late_weights, w2_loaded)
            steps(BOTH, 1, first_f=True)
            with act.Fori(2, GROUPS) as g:
                steps(BOTH, g)
            steps(LAST, GROUPS)

        @block.vector
        def _(dve):
            v = nc.vector
            chain_a = Chain(dve, dve_a, A_LINKS)
            chain_m = Chain(dve, dve_m, M_LINKS)

            def split_weights(weights, first):
                for n, (_, dst, stage) in enumerate(weights):
                    dve.wait_ge(w_hi, first + n + 1)
                    v.tensor_tensor(dst[1][:], stage, dst[0][:], ALU.subtract).then_inc(w_lo, 1)

            def layernorm(src, chain, ready):
                for t in range(TT):
                    last = v.bn_stats(stats[:, t, :], src[:, t, :])
                chain.link(last)
                hold(dve)
                for t in range(TT):
                    last = v.bn_aggr(moments[:, t, :], stats[:, t, :])
                chain.link(last)
                ve, y, w = nt[:, 0, :], nt[:, 1, :], nt[:, 2, :]
                chain.link(v.tensor_scalar(ve, moments[:, :, 1], EPS, None, ALU.add))
                chain.link(v.tensor_scalar(y.bitcast(I32), ve.bitcast(I32), 1, None, ALU.logical_shift_right))
                chain.link(v.tensor_scalar(y.bitcast(I32), y.bitcast(I32), -1.0, float(RSQRT_MAGIC), ALU.mult, ALU.add))
                for _ in range(NEWTON):
                    chain.link(v.tensor_tensor(w, y, y, ALU.mult))
                    chain.link(v.tensor_tensor(w, w, ve, ALU.mult))
                    chain.link(v.tensor_scalar(w, w, -0.5, 1.5, ALU.mult, ALU.add))
                    chain.link(v.tensor_tensor(y, y, w, ALU.mult))
                for t in range(TT):
                    last = v.tensor_scalar(xn[:, t, :], src[:, t, :], moments[:, t, 0:1], nt[:, 1, t:t + 1], ALU.subtract, ALU.mult)
                last.then_inc(ready, 1)

            def lo_part(s, g, hi_sem, hi_count, dst, hi):
                b = fill(s)[0]
                dve.wait_ge(hi_sem, hi_count)
                v.tensor_tensor(dst, bank[b][:], hi, ALU.subtract).then_inc(taken[b], 1)

            def wide(t2):
                return t2.unsqueeze(2).to_broadcast([P, TT, EXPERTS])

            def route():
                link = chain_m.link
                mx, sm, rs, m1, k1, m2, k2 = (tk[:, i, :] for i in range(7))
                link(v.tensor_reduce(mx, lg[:], AX.X, ALU.max))
                v.tensor_tensor(lg[:], lg[:], wide(mx), ALU.subtract).then_inc(logits_shifted, 1)
                dve.wait_ge(exp_ready, chain_m.group + 1)
                link(v.tensor_reduce(sm, pr[:], AX.X, ALU.add))
                link(v.reciprocal(rs, sm))
                link(v.tensor_tensor(pr[:], pr[:], wide(rs), ALU.mult))
                link(v.tensor_reduce(m1, pr[:], AX.X, ALU.max))
                for m, k, one, p in ((m1, k1, one1, pr), (m2, k2, one2, pr2)):
                    if p is pr2:
                        link(v.scalar_tensor_tensor(out=pr2[:].rearrange("p t e -> p (t e)"), in0=one1[:].rearrange("p t e -> p (t e)"),
                                                    scalar=-2.0, in1=pr[:].rearrange("p t e -> p (t e)"), op0=ALU.mult, op1=ALU.add))
                        link(v.tensor_reduce(m2, pr2[:], AX.X, ALU.max))
                    link(v.tensor_tensor(key[:], p[:], wide(m), ALU.is_ge))
                    link(v.tensor_tensor(key[:], key[:], rank_sb[:].unsqueeze(1).to_broadcast([P, TT, EXPERTS]), ALU.mult))
                    link(v.tensor_reduce(k, key[:], AX.X, ALU.max))
                    link(v.tensor_tensor(one[:], key[:], wide(k), ALU.is_equal))
                link(v.tensor_tensor(gate_val[:], m1, m2, ALU.add))
                v.tensor_scalar(gate_val[:], gate_val[:], tanh_g[:, 1:2], None, ALU.mult)
                link(v.tensor_tensor(one2[:], one2[:], one1[:], ALU.subtract))
                for one, dst in ((one1, a_first), (one2, a_diff)):
                    last = v.tensor_tensor(dst.rearrange("p t (e r) -> p (t e) r", e=EXPERTS),
                                           a_all.rearrange("p t (e r) -> p (t e) r", e=EXPERTS),
                                           one[:].rearrange("p t e -> p (t e)").unsqueeze(2).to_broadcast([P, TT * EXPERTS, RANK]), ALU.mult)
                last.then_inc(routed, 1)

            HI_A, HI_M = 6, 6

            def step(s, g, f, first, first_f):
                kind = s[0]
                if kind == "ln1":
                    dve.wait_ge(x_loaded, 16 * (g + 1))
                    layernorm(xin, chain_a, xn1_ready)
                elif kind == "xT":
                    lo_part(s, g, hi_a, g * HI_A + s[1] + 1, xT_lo[:, s[1], :], xT_hi[:, s[1], :])
                elif kind == "q":
                    lo_part(s, g, hi_a, g * HI_A + 2 + s[1] + 1, q_lo[:, s[1], :], q_hi[:, s[1], :])
                elif kind == "k":
                    lo_part(s, g, hi_a, g * HI_A + 4 + s[1] + 1, k_lo[:, s[1], :], k_hi[:, s[1], :])
                elif kind == "S":
                    _, bt, quad, part = s
                    b = fill(s)[0]
                    wait_full(dve, s, g)
                    width = P if part == 0 else SEQ
                    h0 = 4 * quad + (0 if part == 0 else 2 * part - 2)
                    n = 512 // width
                    v.tensor_reduce(neg_max[:, bt, min(part, 1), h0:h0 + n], bank[b][:].rearrange("p (n w) -> p n w", w=width),
                                    AX.X, ALU.max, negate=True).then_inc(taken[b], 1)
                elif kind == "norm":
                    _, b, pr_ = s
                    n = 2 * b + pr_
                    wait_full(dve, ("AV", b, pr_), g)
                    hold(dve)
                    chain_a.link(v.stream_shuffle(denom[:], bank[3][:], [HD + i % HD for i in range(HSLOT)]))
                    chain_a.link(v.reciprocal(denom[:], denom[:]))
                    wait_earlier(dve, att_ready, g, 4, n, first)
                    v.tensor_tensor(att[:].rearrange("p a t -> p (a t)"), bank[3][:], denom[:], ALU.mult).then_inc(taken[3], 1)
                elif kind == "wo":
                    b = fill(s)[0]
                    wait_full(dve, s, f)
                    v.scalar_tensor_tensor(out=x1[:, 2 * s[1]:2 * s[1] + 2, :].rearrange("p t d -> p (t d)"), in0=bank[b][:],
                                           scalar=tanh_g[:, 0:1], in1=xres[:, 2 * s[1]:2 * s[1] + 2, :].rearrange("p t d -> p (t d)"),
                                           op0=ALU.mult, op1=ALU.add).then_inc(taken[b], 1)
                elif kind == "ln2":
                    wait_taken(dve, ("wo", 0), f)
                    wait_taken(dve, ("wo", 1), f)
                    layernorm(x1, chain_m, xn2_ready)
                elif kind == "x2T":
                    lo_part(s, f, hi_m, f * HI_M + s[1] + 1, xT_lo[:, s[1], :], xT_hi[:, s[1], :])
                elif kind == "ag":
                    b = fill(s)[0]
                    dve.wait_ge(hi_m, f * HI_M + 2 + s[1] + 1)
                    v.tensor_tensor(lg[:, 2 * s[1]:2 * s[1] + 2, :], bank[b][:].rearrange("p (t c) -> p t c", t=2)[:, :, P:NAG],
                                    gb_sb[:].unsqueeze(1).to_broadcast([P, 2, EXPERTS]), ALU.add).then_inc(taken[b], 1)
                elif kind == "route":
                    wait_taken(dve, ("ag", 0), f)
                    wait_taken(dve, ("ag", 1), f)
                    route()
                elif kind == "aT":
                    lo_part(s, f, hi_m, f * HI_M + 4 + s[1] + 1, (a1_lo, a2_lo)[s[1]][:, 0, :], (a1_hi, a2_hi)[s[1]][:, 0, :])
                elif kind == "up2":
                    c = s[1]
                    wait_taken(dve, s, f)
                    wait_earlier(dve, h_ready, f, CHUNKS, c - 1, first_f)
                    v.tensor_tensor(relu_sum[:, c % 2, :], relu1[:, c % 2, :], relu2, ALU.add).then_inc(sum_ready, 1)
                elif kind == "out":
                    p = s[1]
                    wait_full(dve, ("down", p), f)
                    if not first_f:
                        dve.wait_ge(out_stored, f * 32)
                    ins = v.tensor_tensor(fin[:, 2 * p:2 * p + 2, :], bank[6 + p][:].rearrange("p (t d) -> p t d", t=2),
                                          bo2[:].unsqueeze(1).to_broadcast([P, 2, D]), ALU.add)
                    ins.then_inc(taken[6 + p], 1)
                    wait_taken(dve, ("down", p), f)
                    for t in (2 * p, 2 * p + 1):
                        last = v.scalar_tensor_tensor(out=fin[:, t, :], in0=fin[:, t, :], scalar=gate_val[:, t:t + 1],
                                                      in1=x1[:, t, :], op0=ALU.mult, op1=ALU.add)
                    last.then_inc(out_ready, 1)

            def steps(todo, g, first=False, first_f=False):
                chain_a.start(g)
                chain_m.start(g - 1)
                for s in todo:
                    step(s, g, g - 1, first, first_f)
                assert chain_a.n in (0, A_LINKS) and chain_m.n in (0, M_LINKS), (chain_a.n, chain_m.n)

            v.memset(v_ones[:], 1.0)
            for e in range(EXPERTS):
                v.memset(rank_sb[:, e:e + 1], float(EXPERTS - e))
            for half in (32, 96):
                last = v.memset(k_stack[half:half + 32, :, :].bitcast(F32), 1.0)
            last.then_inc(consts, 1)
            split_weights(first_weights, 0)
            dve.wait_ge(small_loaded, 16 * NSMALL)
            v.tensor_scalar(bo2[:], bo2[:], 2.0, None, ALU.mult).then_inc(dve_setup, 1)
            dve.wait_ge(dve_setup, 1)
            dve.wait_ge(tanh_ready, 1)
            steps(ATTENTION, 0, first=True)
            split_weights(late_weights, NW)
            steps(BOTH, 1, first_f=True)
            with dve.Fori(2, GROUPS) as g:
                steps(BOTH, g)
            steps(LAST, GROUPS)

        @block.gpsimd
        def _(pool):
            p_ = nc.gpsimd

            def step(s, g, f, first, first_f):
                kind = s[0]
                if kind == "cx":
                    pool.wait_ge(c_hi_ready, g + 1)
                    p_.tensor_tensor(c_lo[:], cin[:], c_hi[:], ALU.subtract).then_inc(c_lo_ready, 1)
                elif kind == "xres":
                    pool.wait_ge(x_loaded, 16 * (g + 1))
                    if not first:
                        wait_taken(pool, ("wo", 1), f)
                    hold(pool)
                    p_.tensor_copy(xres[:], xin[:]).then_inc(xres_ready, 1)
                elif kind == "ST":
                    _, b, quad, part = s
                    wait_taken(pool, s, g)
                    hold(pool)
                    n, width = (4, P) if part == 2 else (2, SEQ)
                    blk = probs[:, (b * QUADS + quad) % 2, part, :].rearrange("p (n w) -> p n w", n=n)[:, :, 0:P]
                    p_.affine_select(out=blk, in_=blk, pattern=[[0, n], [1, P]], compare_op=ALU.is_ge, fill=0.0,
                                     base=0, channel_multiplier=-1).then_inc(masked, 1)
                elif kind == "norm":
                    _, b, pr_ = s
                    n = 2 * b + pr_
                    pool.wait_ge(att_hi_ready, g * 4 + n + 1)
                    where = (slice(None), slice(2 * pr_, 2 * pr_ + 2), slice(b * SEQ, (b + 1) * SEQ))
                    p_.tensor_tensor(att_lo[where], att[:], att_hi[where], ALU.subtract).then_inc(att_ready, 1)
                elif kind == "split":
                    c = s[1]
                    pool.wait_ge(h_hi_ready, f * CHUNKS + c + 1)
                    p_.tensor_tensor(h_lo[:, c % 2, :], relu_sum[:, c % 2, :], h_hi[:, c % 2, :], ALU.subtract).then_inc(h_ready, 1)

            def steps(todo, g, first=False, first_f=False):
                for s in todo:
                    step(s, g, g - 1, first, first_f)

            p_.memset(ident[:], 0.0)
            p_.memset(causal[:], 0.0).then_inc(pool_step, 1)
            pool.wait_ge(pool_step, 1)
            p_.affine_select(out=ident[:], in_=ident[:], pattern=[[-1, P]], compare_op=ALU.not_equal, fill=1.0,
                             base=0, channel_multiplier=1)
            p_.affine_select(out=causal[:], in_=causal[:], pattern=[[0, 4], [-1, P]], compare_op=ALU.is_ge, fill=MASKED,
                             base=0, channel_multiplier=1).then_inc(pool_step, 1)
            pool.wait_ge(pool_step, 2)
            p_.tensor_copy(ident_b[:], ident[:]).then_inc(consts, 1)
            steps(ATTENTION, 0, first=True)
            steps(BOTH, 1, first_f=True)
            with pool.Fori(2, GROUPS) as g:
                steps(BOTH, g)
            steps(LAST, GROUPS)


def kernel(x, ctx_1024, g_xattn, g_ffn, L0_xattn_wq, L0_xattn_wk, L0_xattn_wv, L0_xattn_wo, L0_ffn_wi, L0_ffn_bi,
           L0_ffn_wo, L0_ffn_bo, L0_ffn_lora_A, L0_ffn_lora_B, L0_ffn_gate_w, L0_ffn_gate_b):
    import concourse.bacc as bacc
    from concourse.bass_utils import run_bass_kernel_spmd

    def lay(a):
        return np.ascontiguousarray(a)

    x = np.asarray(x)
    wo_t = np.asarray(L0_xattn_wo).T.reshape(HEADS, HD, D)
    wo_padded = np.zeros((HEADS, HSLOT, D), wo_t.dtype)
    wo_padded[:, :HD] = wo_t
    arrays = {
        "x": lay(x.reshape(BATCH * SEQ, D)),
        "ctxT": lay(np.asarray(ctx_1024).reshape(BATCH * SEQ, D).T),
        "g_xattn": lay(g_xattn),
        "g_ffn": lay(g_ffn),
        "wqT": lay(np.asarray(L0_xattn_wq).T),
        "wkT": lay(np.asarray(L0_xattn_wk).T),
        "wvT": lay(np.asarray(L0_xattn_wv).T),
        "woT": wo_padded.reshape(HEADS * HSLOT, D),
        "wiT": lay(np.asarray(L0_ffn_wi).T),
        "bi": lay(np.asarray(L0_ffn_bi).reshape(CHUNKS, P).T),
        "w2T": lay(np.asarray(L0_ffn_wo).T),
        "bo": lay(L0_ffn_bo),
        "abT": lay(np.concatenate([np.asarray(L0_ffn_lora_A).reshape(EXPERTS * RANK, D), np.asarray(L0_ffn_gate_w)]).T),
        "bT": lay(np.asarray(L0_ffn_lora_B).transpose(0, 2, 1).reshape(EXPERTS * RANK, FF)),
        "gate_b": lay(L0_ffn_gate_b),
    }
    nc = bacc.Bacc("TRN2", target_bir_lowering=False, num_devices=1)
    args = [nc.dram_tensor(f"in_{n}", a.shape, mybir.dt.from_np(a.dtype), kind="ExternalInput").ap() for n, a in arrays.items()]
    out = nc.dram_tensor("out", (BATCH * SEQ, D), F32, kind="ExternalOutput").ap()
    flamingo_layer(nc, *args, out)
    r = run_bass_kernel_spmd(nc, [{f"in_{n}": a for n, a in arrays.items()}], core_ids=[0])
    return r.results[0]["out"].reshape(BATCH, SEQ, D)
```

```python
from contextlib import ExitStack

import numpy as np
import concourse.bass as bass
from concourse import mybir

F32 = mybir.dt.float32
F32R = mybir.dt.float32r
BF16 = mybir.dt.bfloat16
I32 = mybir.dt.int32
ALU = mybir.AluOpType
ACT = mybir.ActivationFunctionType
AX = mybir.AxisListType

P = 128
BATCH, SEQ, D = 16, 256, 256
HEADS, HD = 16, 16
FF, EXPERTS, RANK = 1024, 8, 16
EPS = 1e-5
GB = 2
GT = GB * SEQ
GROUPS = BATCH // GB
TT = GT // P
DK = D // P
QUADS = HEADS // 4
HSLOT = 32
CHUNKS = FF // P
NAG = EXPERTS * RANK + EXPERTS
SPLITS = 3
SROWS = SPLITS * HD
HALF = 8
SCALE = 1.0 / float(np.sqrt(HD))
MASKED = -1e30
RSQRT_MAGIC = 0x5F3759DF


def plan(fills):
    count, where = {}, {}
    for name, bank in fills:
        where[name] = (bank, count.get(bank, 0))
        count[bank] = count.get(bank, 0) + 1
    return where, count


FRONT = [("k", 0), ("k", 1), ("xT", 0), ("xT", 1), ("q", 0), ("q", 1), ("v", 0), ("v", 1)]
SCORES = []
for _b in range(GB):
    SCORES += [("S", _b, _q, _p) for _q in range(QUADS) for _p in range(3)] + [("mT", _b)]
PROBS = []
for _u in range(GB * QUADS + 1):
    if _u < GB * QUADS:
        PROBS += [("ST", _u // QUADS, _u % QUADS, _p) for _p in range(3)]
    if _u > 0:
        _v = _u - 1
        PROBS += [("AV", _v // QUADS, _v % QUADS)]
        if _v % 2:
            PROBS += [("raw", _v // QUADS, (_v % QUADS) // 2)]
    if _u == QUADS + 1:
        PROBS += [("oT", 0), ("oT", 1)]
    if _u == QUADS + 2:
        PROBS += [("nT", 0), ("next ln1",), ("next cx",)]
TAIL = [("oT", 2), ("oT", 3), ("nT", 1)]
FFN = []
for _c in range(CHUNKS + 3):
    if _c < CHUNKS:
        FFN.append(("up1", _c))
    if 0 <= _c - 1 < CHUNKS:
        FFN.append(("up2", _c - 1))
    if 0 <= _c - 2 < CHUNKS:
        FFN.append(("split", _c - 2))
    if 0 <= _c - 3 < CHUNKS:
        FFN.append(("down", _c - 3))
FFN += [("out", 0), ("out", 1)]
MID = [("wo", 0), ("wo", 1), ("ln2",), ("x2T", 0), ("x2T", 1), ("ag", 0), ("ag", 1), ("route",), ("aT", 0), ("aT", 1)]

_rot = [s for s in FRONT + SCORES + PROBS + TAIL if s[0] not in ("AV", "raw", "next ln1", "next cx")]
A_FILLS, A_COUNT = plan([(s, n % 3) for n, s in enumerate(_rot)]
                        + [(("AV", b, pair), 3) for b in range(GB) for pair in range(QUADS // 2)])
M_FILLS, M_COUNT = plan([(("wo", 0), 4), (("wo", 1), 5), (("x2T", 0), 6), (("x2T", 1), 7), (("ag", 0), 4),
                         (("ag", 1), 5), (("aT", 0), 6), (("aT", 1), 7)]
                        + [f for c in range(CHUNKS) for f in ((("up1", c), 4 + c % 2), (("up2", c), 4 + c % 2))]
                        + [(("down", 0), 6), (("down", 1), 7)])


def merge(a, b):
    out, i, j = [], 0, 0
    while i < len(a) or j < len(b):
        if j >= len(b) or (i < len(a) and i * len(b) <= j * len(a)):
            out.append(a[i])
            i += 1
        else:
            out.append(b[j])
            j += 1
    return out


def without(steps, *kinds):
    return [s for s in steps if s[0] not in kinds]


ATTENTION = FRONT + SCORES + PROBS + TAIL
BOTH = ([("k", 0), ("k", 1), ("xT", 0), ("xT", 1), ("q", 0), ("q", 1), ("wo", 0), ("wo", 1), ("v", 0), ("v", 1),
         ("ln2",)] + SCORES[:3] + [("x2T", 0), ("x2T", 1)] + SCORES[3:5] + [("ag", 0), ("ag", 1)] + SCORES[5:7]
        + [("route",)] + SCORES[7:10] + [("aT", 0), ("aT", 1)]
        + merge(SCORES[10:] + PROBS, FFN[:-4]) + TAIL[:2] + FFN[-4:-3] + TAIL[2:] + FFN[-3:])
BOTH_LAST = without(BOTH, "next ln1", "next cx")
LAST = MID + FFN
M_KINDS = {s[0] for s in MID + FFN}

NEWTON = 3
LN_LINKS = 5 + 4 * NEWTON
ROUTE_LINKS = 17
A_LINKS = LN_LINKS + TT
M_LINKS = LN_LINKS + ROUTE_LINKS
STACK_DMAS = SPLITS * DK


class Chain:

    def __init__(self, eng, sem, per):
        self.eng, self.sem, self.per, self.n, self.group = eng, sem, per, 0, 0

    def start(self, group):
        self.group, self.n = group, 0

    def link(self, ins):
        self.n += 1
        ins.then_inc(self.sem, 1)
        self.eng.wait_ge(self.sem, self.group * self.per + self.n)


def flamingo_layer(nc, x, ctxT, g_xattn, g_ffn, wqT, wkT, wvT, woT, wiT, bi, w2T, bo, abT, bT, gate_b, out):
    with ExitStack() as ctx:
        def sb(name, shape, dt):
            return ctx.enter_context(nc.sbuf_tensor(name, shape, dt))

        def sem(name):
            return ctx.enter_context(nc.semaphore(name))

        bank = [ctx.enter_context(nc.psum_tensor(f"bank{i}", [P, 512], F32)) for i in range(8)]

        def pair(name, n, cols):
            return sb(name + "_hi", [P, n, cols], F32R), sb(name + "_lo", [P, n, cols], F32R)

        wq, wk, wv = pair("wq", DK, D), pair("wk", DK, D), pair("wv", DK, D)
        wo = pair("wo", DK, D)
        ab = pair("ab", DK, NAG)
        wb = pair("wb", 1, FF)
        wi = pair("wi", DK, FF)
        w2 = pair("w2", CHUNKS, D)
        bi_sb = sb("bi_sb", [P, CHUNKS], F32)
        bo2 = sb("bo2", [P, D], F32)
        gb_sb = sb("gb_sb", [P, EXPERTS], F32)
        rank_sb = sb("rank_sb", [P, EXPERTS], F32)
        gates = sb("gates", [P, 2], F32)
        tanh_g = sb("tanh_g", [P, 2], F32)
        ident = sb("ident", [P, P], F32)
        ident_b = sb("ident_b", [P, P], BF16)
        causal = sb("causal", [P, 4, P], BF16)

        xin = sb("xin", [P, TT, D], F32)
        cin = sb("cin", [P, DK, GT], F32)
        c_hi, c_lo = pair("c", DK, GT)
        xn = sb("xn", [P, TT, D], F32)
        xT_hi, xT_lo = pair("xT", DK, GT)
        scratch = sb("scratch", [P, 4096], F32)
        compact = scratch[:, :].bitcast(F32R).rearrange("p (o s m t) -> p o s m t", o=2, s=2, m=DK)
        q_hi, q_lo, k_hi, k_lo = (compact[:, i // 2, i % 2] for i in range(4))
        probs = scratch[:, 0:3072].rearrange("p (s a t) -> p s a t", s=2, a=3)
        q_stack = sb("q_stack", [P, HALF, GT], F32R)
        k_stack = sb("k_stack", [P, HALF, GT], F32R)
        v_ones = sb("v_ones", [P, TT, HEADS, HSLOT], F32)
        neg_max = sb("neg_max", [P, GB, 2, HEADS], F32)
        max_row = sb("max_row", [2 * HEADS, GB, P], F32R)
        inv_sum = sb("inv_sum", [P, TT, HEADS], F32)
        raw = sb("raw", [P, QUADS, GT], F32)
        att = sb("att", [P, TT, HEADS, HD], F32)
        att_hi, att_lo = pair("att", DK, GT)

        work = sb("work", [P, 5120], F32)
        x1 = work[:, 0:1024].rearrange("p (t d) -> p t d", t=TT)
        fin = work[:, 1024:2048].rearrange("p (t d) -> p t d", t=TT)
        a_all = work[:, 2048:2560].rearrange("p (t e) -> p t e", t=TT)
        a_first = work[:, 2560:3072].rearrange("p (t e) -> p t e", t=TT)
        a_diff = work[:, 3072:3584].rearrange("p (t e) -> p t e", t=TT)
        relu1 = work[:, 3584:4608].rearrange("p (s t) -> p s t", s=2)
        relu2 = work[:, 4608:5120]
        relu_sum = work[:, 2048:3072].rearrange("p (s t) -> p s t", s=2)
        a1_hi, a1_lo = pair("a1", 1, GT)
        a2_hi, a2_lo = pair("a2", 1, GT)
        h_hi, h_lo = pair("h", 2, GT)
        stats = sb("stats", [P, TT, 6], F32)
        moments = sb("moments", [P, TT, 2], F32)
        nt = sb("nt", [P, 3, TT], F32)
        lg = sb("lg", [P, TT, EXPERTS], F32)
        pr = sb("pr", [P, TT, EXPERTS], F32)
        pr2 = sb("pr2", [P, TT, EXPERTS], F32)
        key = sb("key", [P, TT, EXPERTS], F32)
        one1 = sb("one1", [P, TT, EXPERTS], F32)
        one2 = sb("one2", [P, TT, EXPERTS], F32)
        tk = sb("tk", [P, 8, TT], F32)
        gate_val = sb("gate_val", [P, TT], F32)

        full = [sem(f"full{i}") for i in range(8)]
        taken = [sem(f"taken{i}") for i in range(8)]
        w_loaded = sem("w_loaded")
        small_loaded = sem("small_loaded")
        w2_loaded = sem("w2_loaded")
        w_hi = sem("w_hi")
        w_lo = sem("w_lo")
        consts = sem("consts")
        pool_step = sem("pool_step")
        tanh_ready = sem("tanh_ready")
        x_loaded = sem("x_loaded")
        c_loaded = sem("c_loaded")
        c_hi_ready = sem("c_hi_ready")
        c_lo_ready = sem("c_lo_ready")
        xn1_ready = sem("xn1_ready")
        res_loaded = sem("res_loaded")
        hi_a = sem("hi_a")
        hi_m = sem("hi_m")
        q_stacked = sem("q_stacked")
        k_stacked = sem("k_stacked")
        spilled = [sem("q_spilled"), sem("k_spilled")]
        max_stacked = [sem(f"max_stacked{b}") for b in range(GB)]
        masked = sem("masked")
        av_done = sem("av_done")
        xn2_ready = sem("xn2_ready")
        logits_shifted = sem("logits_shifted")
        exp_ready = sem("exp_ready")
        routed = sem("routed")
        sum_ready = sem("sum_ready")
        h_hi_ready = sem("h_hi_ready")
        h_ready = sem("h_ready")
        down_done = sem("down_done")
        out_ready = sem("out_ready")
        out_stored = sem("out_stored")
        dve_a = sem("dve_a")
        dve_m = sem("dve_m")
        dve_0 = sem("dve_0")
        dve_setup = sem("dve_setup")
        held = sem("held")

        def fill(step):
            where, count = (M_FILLS, M_COUNT) if step[0] in M_KINDS else (A_FILLS, A_COUNT)
            b, n = where[step]
            return b, n, count[b]

        def wait_full(eng, step, g):
            b, n, per = fill(step)
            eng.wait_ge(full[b], g * per + n + 1)

        def wait_taken(eng, step, g):
            b, n, per = fill(step)
            eng.wait_ge(taken[b], g * per + n + 1)

        def wait_free(eng, step, g, first):
            b, n, per = fill(step)
            if not first or n > 0:
                eng.wait_ge(taken[b], g * per + n)

        def wait_earlier(eng, s, g, per, n, first):
            if not first or n > 0:
                eng.wait_ge(s, g * per + n)

        def hold(eng):
            eng.sem_inc(held, 1)

        first_weights = []
        at = 0
        for dram, dst in ((wqT, wq), (wkT, wk), (wvT, wv), (woT, wo), (abT, ab), (bT, wb)):
            n, cols = dst[0].shape[1], dst[0].shape[2]
            first_weights.append((dram.rearrange("(n p) c -> p n c", p=P), dst,
                                  scratch[:, at:at + n * cols].rearrange("p (n c) -> p n c", n=n)))
            at += n * cols
        late_weights = []
        at = 0
        for dram, dst in ((wiT, wi), (w2T, w2)):
            n, cols = dst[0].shape[1], dst[0].shape[2]
            late_weights.append((dram.rearrange("(n p) c -> p n c", p=P), dst,
                                 work[:, at:at + n * cols].rearrange("p (n c) -> p n c", n=n)))
            at += n * cols
        NW = len(first_weights)
        NSMALL = 5

        x_rows = x.rearrange("(g t p) d -> g p t d", p=P, t=TT)
        out_rows = out.rearrange("(g t p) d -> g p t d", p=P, t=TT)
        c_cols = ctxT.rearrange("(n p) (g t) -> g p n t", p=P, g=GROUPS)

        heads_dram = nc.dram_tensor("heads_dram", (2, DK, 2, P, GT), F32, kind="Internal").ap()

        block = ctx.enter_context(nc.Block())

        @block.sync
        def _(sp):
            def load_group(g, first):
                if not first:
                    sp.wait_ge(c_lo_ready, g)
                    sp.wait_ge(xn1_ready, g)
                sp.dma_start(xin[:], x_rows[g]).then_inc(x_loaded, 16)
                sp.dma_start(cin[:], c_cols[g]).then_inc(c_loaded, 16)

            def spill(o, m):
                sp.dma_start(heads_dram[o, m].rearrange("s p t -> p s t"),
                             compact[:, o, :, m, :].bitcast(F32)).then_inc(spilled[o], 16)

            def stack(o, m, pieces, dst, s):
                for i, part in enumerate(pieces):
                    sp.dma_start(dst[64 * m + HD * i:64 * m + HD * (i + 1), :, :].bitcast(F32),
                                 heads_dram[o, m, part].rearrange("(h d) t -> d h t", d=HD)).then_inc(s, 16)

            def stack_max(g, b):
                wait_taken(sp, ("mT", b), g)
                for qt in range(2):
                    for m in range(DK):
                        row, head = 64 * m + SROWS, qt * HEADS + m * HALF
                        sp.dma_start(q_stack[row:row + 1, :, b * SEQ + qt * P:b * SEQ + (qt + 1) * P].bitcast(F32),
                                     max_row[head:head + HALF, b, :].bitcast(F32)).then_inc(max_stacked[b], 16)

            def store(f):
                for p in range(2):
                    sp.wait_ge(out_ready, f * 2 + p + 1)
                    sp.dma_start(out_rows[f][:, 2 * p:2 * p + 2, :], fin[:, 2 * p:2 * p + 2, :]).then_inc(out_stored, 16)

            def load_residual(g):
                sp.dma_start(x1, x_rows[g]).then_inc(res_loaded, 16)

            def group(g, load_next=True, store_last=True):
                for o, name, pieces, dst, s in ((1, "k", (0, 1, 0), k_stack, k_stacked), (0, "q", (0, 0, 1), q_stack, q_stacked)):
                    for m in range(DK):
                        wait_taken(sp, (name, m), g)
                        spill(o, m)
                    sp.wait_ge(spilled[o], (g + 1) * 16 * DK)
                    for m in range(DK):
                        stack(o, m, pieces, dst, s)
                if load_next:
                    load_group(g + 1, False)
                for b in range(GB):
                    stack_max(g, b)
                if not store_last:
                    sp.wait_ge(w_lo, NW + len(late_weights))
                if store_last:
                    store(g - 1)
                load_residual(g)

            load_group(0, True)
            for src, _, stage in first_weights:
                sp.dma_start(stage, src).then_inc(w_loaded, 16)
            sp.dma_start(gates[:, 0:1], g_xattn.rearrange("(a b) -> a b", a=1).partition_broadcast(P)).then_inc(small_loaded, 16)
            sp.dma_start(gates[:, 1:2], g_ffn.rearrange("(a b) -> a b", a=1).partition_broadcast(P)).then_inc(small_loaded, 16)
            sp.dma_start(bi_sb[:], bi).then_inc(small_loaded, 16)
            sp.dma_start(bo2[:], bo.rearrange("(a b) -> a b", a=1).partition_broadcast(P)).then_inc(small_loaded, 16)
            sp.dma_start(gb_sb[:], gate_b.rearrange("(a b) -> a b", a=1).partition_broadcast(P)).then_inc(small_loaded, 16)
            for src, _, stage in late_weights:
                sp.dma_start(stage, src).then_inc(w2_loaded, 16)
            sp.wait_ge(consts, 1)
            group(0, store_last=False)
            with sp.Fori(1, GROUPS - 1) as g:
                group(g)
            group(GROUPS - 1, load_next=False)
            store(GROUPS - 1)
            sp.wait_ge(out_stored, 32 * GROUPS)

        @block.tensor
        def _(pe):
            def mm(*a, **k):
                return nc.tensor.matmul(*a, **k)

            def products(dst, lhs, rhs, tiles, more=False):
                todo = [(i, a, b) for i in range(tiles) for a, b in ((0, 0), (0, 1), (1, 0))]
                for n, (i, a, b) in enumerate(todo):
                    last = mm(dst, lhs[a](i), rhs[b](i), start=(n == 0 and not more), stop=(n == len(todo) - 1),
                              skip_group_check=more)
                return last

            def cols(pair_, lo, n):
                return [lambda i, t=t: t[:, i, lo:lo + n] for t in pair_]

            def step(s, g, f, first, first_f):
                kind = s[0]
                if kind in ("next cx", "next ln1", "ln2", "route", "split", "raw", "out"):
                    return
                if kind not in ("AV", "down"):
                    wait_free(pe, s, f if kind in M_KINDS else g, first_f if kind in M_KINDS else first)
                    ps = bank[fill(s)[0]]
                if kind == "xT":
                    if s[1] == 0:
                        pe.wait_ge(xn1_ready, g + 1)
                    for t in range(TT):
                        last = nc.tensor.transpose(ps[:, t * P:(t + 1) * P], xn[:, t, s[1] * P:(s[1] + 1) * P], ident[:])
                elif kind == "q":
                    if s[1] == 0:
                        wait_taken(pe, ("xT", 0), g)
                        wait_taken(pe, ("xT", 1), g)
                    last = products(ps[:], cols(wq, s[1] * P, P), cols((xT_hi, xT_lo), 0, GT), DK)
                elif kind == "k":
                    if s[1] == 0:
                        pe.wait_ge(c_hi_ready, g + 1)
                        pe.wait_ge(c_lo_ready, g + 1)
                    last = products(ps[:], cols(wk, s[1] * P, P), cols((c_hi, c_lo), 0, GT), DK)
                elif kind == "v":
                    for i in range(2):
                        last = products(ps[:, i * D:(i + 1) * D], cols((c_hi, c_lo), (2 * s[1] + i) * P, P), cols(wv, 0, D), DK)
                elif kind == "S":
                    _, b, quad, part = s
                    if (b, quad, part) == (0, 0, 0):
                        pe.wait_ge(q_stacked, (g + 1) * 16 * STACK_DMAS)
                        pe.wait_ge(k_stacked, (g + 1) * 16 * STACK_DMAS)
                    rows = slice(64 * (quad // 2), 64 * (quad // 2) + SROWS)
                    heads = range(4) if part == 0 else range(2 * part - 2, 2 * part)
                    width = P if part == 0 else SEQ
                    q0 = b * SEQ + (0 if part == 0 else P)
                    for n, j in enumerate(heads):
                        h = 4 * (quad % 2) + j
                        mm(ps[:, n * width:(n + 1) * width], q_stack[rows, h, q0:q0 + P],
                           k_stack[rows, h, b * SEQ:b * SEQ + width], start=(n == 0), stop=False, skip_group_check=True)
                    edge = ps[:].rearrange("p (n w) -> p n w", w=width)[:, :, width - P:width]
                    last = mm(edge, ident_b[:], causal[:, 0:len(heads), :], start=False, stop=True, skip_group_check=True)
                elif kind == "mT":
                    wait_taken(pe, ("S", s[1], QUADS - 1, 2), g)
                    last = nc.tensor.transpose(ps[0:2 * HEADS, 0:P], neg_max[:, s[1]].rearrange("p a h -> p (a h)"), ident[:])
                elif kind == "ST":
                    _, b, quad, part = s
                    if (quad, part) == (0, 0):
                        pe.wait_ge(max_stacked[b], (g + 1) * 64)
                    rows = slice(64 * (quad // 2), 64 * (quad // 2) + SROWS + 1)
                    heads = range(4) if part == 2 else range(2 * part, 2 * part + 2)
                    width = P if part == 2 else SEQ
                    k0 = b * SEQ + (P if part == 2 else 0)
                    for n, j in enumerate(heads):
                        h = 4 * (quad % 2) + j
                        last = mm(ps[:, n * width:(n + 1) * width], k_stack[rows, h, k0:k0 + P],
                                  q_stack[rows, h, (b + 1) * SEQ - width:(b + 1) * SEQ], start=True, stop=True)
                elif kind == "AV":
                    _, b, quad = s
                    u = b * QUADS + quad
                    pe.wait_ge(masked, g * 3 * GB * QUADS + 3 * (u + 1))
                    ps = bank[3]
                    if quad % 2 == 0:
                        wait_free(pe, ("AV", b, quad // 2), g, first)
                    c0 = (quad % 2) * SEQ
                    for kt in range(2):
                        for j in range(4):
                            src = probs[:, u % 2, j // 2, (j % 2) * SEQ:(j % 2 + 1) * SEQ] if kt == 0 else \
                                probs[:, u % 2, 2, j * P:(j + 1) * P]
                            last = mm(ps[HSLOT * j:HSLOT * (j + 1), c0 + kt * P:c0 + SEQ],
                                      v_ones[:, 2 * b + kt, 4 * quad + j, :], src,
                                      start=(kt == 0), stop=(kt == 1), skip_group_check=True)
                    last.then_inc(full[3] if quad % 2 else av_done, 1)
                    return
                elif kind == "oT":
                    t = s[1]
                    wait_taken(pe, ("AV", t // 2, 1), g)
                    for quad in range(QUADS):
                        last = nc.tensor.transpose(ps[:, quad * P:(quad + 1) * P], raw[:, quad, t * P:(t + 1) * P], ident[:])
                elif kind == "nT":
                    b = s[1]
                    wait_taken(pe, ("oT", 2 * b + 1), g)
                    for m in range(DK):
                        for i in range(2):
                            last = nc.tensor.transpose(ps[:, m * SEQ + i * P:m * SEQ + (i + 1) * P],
                                                       att[:, 2 * b + i, m * HALF:(m + 1) * HALF, :].rearrange("p h d -> p (h d)"), ident[:])
                elif kind == "wo":
                    if s[1] == 0:
                        wait_taken(pe, ("nT", 0), f)
                        wait_taken(pe, ("nT", 1), f)
                    for i in range(2):
                        last = products(ps[:, i * D:(i + 1) * D], cols((att_hi, att_lo), (2 * s[1] + i) * P, P),
                                        cols(wo, 0, D), DK)
                elif kind == "x2T":
                    if s[1] == 0:
                        pe.wait_ge(xn2_ready, f + 1)
                    for t in range(TT):
                        last = nc.tensor.transpose(ps[:, t * P:(t + 1) * P], xn[:, t, s[1] * P:(s[1] + 1) * P], ident[:])
                elif kind == "ag":
                    if s[1] == 0:
                        wait_taken(pe, ("x2T", 0), f)
                        wait_taken(pe, ("x2T", 1), f)
                    for i in range(2):
                        last = products(ps[:, i * D:i * D + NAG], cols((xT_hi, xT_lo), (2 * s[1] + i) * P, P), cols(ab, 0, NAG), DK)
                elif kind == "aT":
                    if s[1] == 0:
                        pe.wait_ge(routed, f + 1)
                    src = (a_first, a_diff)[s[1]]
                    for t in range(TT):
                        last = nc.tensor.transpose(ps[:, t * P:(t + 1) * P], src[:, t, :], ident[:])
                elif kind == "up1":
                    c = s[1]
                    if c == 0:
                        wait_taken(pe, ("aT", 0), f)
                        wait_taken(pe, ("aT", 1), f)
                    products(ps[:], cols(wi, c * P, P), cols((xT_hi, xT_lo), 0, GT), DK)
                    last = products(ps[:], cols(wb, c * P, P), cols((a1_hi, a1_lo), 0, GT), 1, more=True)
                elif kind == "up2":
                    last = products(ps[:], cols(wb, s[1] * P, P), cols((a2_hi, a2_lo), 0, GT), 1, more=True)
                elif kind == "down":
                    c = s[1]
                    pe.wait_ge(h_ready, f * CHUNKS + c + 1)
                    for t in range(TT):
                        p = t // 2
                        if c == 0 and t % 2 == 0:
                            wait_free(pe, ("down", p), f, first_f)
                        dst = bank[6 + p][:, (t % 2) * D:(t % 2 + 1) * D]
                        for n, (a, b) in enumerate(((h_hi, 0), (h_hi, 1), (h_lo, 0))):
                            last = mm(dst, a[:, c % 2, t * P:(t + 1) * P], w2[b][:, c, :],
                                      start=(c == 0 and t % 2 == 0 and n == 0), stop=(c == CHUNKS - 1 and n == 2),
                                      skip_group_check=True)
                        if c == CHUNKS - 1 and t % 2:
                            last.then_inc(full[6 + p], 1)
                    if c < CHUNKS - 1:
                        last.then_inc(down_done, 1)
                    return
                last.then_inc(full[fill(s)[0]], 1)

            def steps(todo, g, first=False, first_f=False):
                for s in todo:
                    step(s, g, g - 1, first, first_f)

            pe.wait_ge(consts, 2)
            pe.wait_ge(w_lo, NW)
            steps(ATTENTION, 0, first=True)
            pe.wait_ge(w_lo, NW + len(late_weights))
            steps(BOTH, 1, first_f=True)
            with pe.Fori(2, GROUPS - 1) as g:
                steps(BOTH, g)
            steps(BOTH_LAST, GROUPS - 1)
            steps(LAST, GROUPS)

        @block.scalar
        def _(act):
            def copy(dst, src):
                return nc.scalar.activation(dst, src, ACT.Copy)

            def split_weights(weights, loaded):
                for n, (_, dst, stage) in enumerate(weights):
                    act.wait_ge(loaded, 16 * len(weights))
                    copy(dst[0][:], stage).then_inc(w_hi, 1)

            def split_context(g):
                act.wait_ge(c_loaded, 16 * (g + 1))
                copy(c_hi[:], cin[:]).then_inc(c_hi_ready, 1)

            def step(s, g, f, first, first_f):
                kind = s[0]
                if kind == "next cx":
                    split_context(g + 1)
                elif kind == "xT":
                    wait_full(act, s, g)
                    copy(xT_hi[:, s[1], :], bank[fill(s)[0]][:]).then_inc(hi_a, 1)
                elif kind in ("q", "k"):
                    wait_full(act, s, g)
                    copy((q_hi if kind == "q" else k_hi)[:, s[1], :], bank[fill(s)[0]][:]).then_inc(hi_a, 1)
                elif kind == "v":
                    wait_full(act, s, g)
                    b = fill(s)[0]
                    for i in range(2):
                        last = copy(v_ones[:, 2 * s[1] + i, :, 0:HD], bank[b][:, i * D:(i + 1) * D].rearrange("p (h d) -> p h d", h=HEADS))
                    last.then_inc(taken[b], 1)
                elif kind == "mT":
                    wait_full(act, s, g)
                    b = fill(s)[0]
                    copy(max_row[:, s[1], :], bank[b][0:2 * HEADS, 0:P]).then_inc(taken[b], 1)
                elif kind == "ST":
                    _, bt, quad, part = s
                    u = bt * QUADS + quad
                    b = fill(s)[0]
                    wait_full(act, s, g)
                    if part == 0:
                        wait_earlier(act, full[3] if quad % 2 else av_done, g, GB * QUADS // 2, u // 2, first)
                    nc.scalar.activation(probs[:, u % 2, part, :], bank[b][:], ACT.Exp, scale=SCALE).then_inc(taken[b], 1)
                elif kind == "raw":
                    _, b, pair_ = s
                    wait_full(act, ("AV", b, pair_), g)
                    copy(raw[:, 2 * pair_:2 * pair_ + 2, b * SEQ:(b + 1) * SEQ],
                         bank[3][:].rearrange("p (q t) -> p q t", q=2)).then_inc(taken[3], 1)
                elif kind == "nT":
                    b = s[1]
                    wait_full(act, s, g)
                    copy(att_hi[:, :, b * SEQ:(b + 1) * SEQ],
                         bank[fill(s)[0]][:].rearrange("p (m t) -> p m t", m=DK)).then_inc(hi_a, 1)
                elif kind == "x2T":
                    wait_full(act, s, f)
                    copy(xT_hi[:, s[1], :], bank[fill(s)[0]][:]).then_inc(hi_m, 1)
                elif kind == "ag":
                    wait_full(act, s, f)
                    copy(a_all[:, 2 * s[1]:2 * s[1] + 2, :],
                         bank[fill(s)[0]][:].rearrange("p (t c) -> p t c", t=2)[:, :, 0:P]).then_inc(hi_m, 1)
                elif kind == "route":
                    act.wait_ge(logits_shifted, f + 1)
                    nc.scalar.activation(pr[:], lg[:], ACT.Exp).then_inc(exp_ready, 1)
                elif kind == "aT":
                    wait_full(act, s, f)
                    copy((a1_hi, a2_hi)[s[1]][:, 0, :], bank[fill(s)[0]][:]).then_inc(hi_m, 1)
                elif kind == "up1":
                    c = s[1]
                    b = fill(s)[0]
                    wait_full(act, s, f)
                    wait_earlier(act, sum_ready, f, CHUNKS, c - 1, first_f)
                    nc.scalar.activation(relu1[:, c % 2, :], bank[b][:], ACT.Relu, bias=bi_sb[:, c:c + 1]).then_inc(taken[b], 1)
                elif kind == "up2":
                    c = s[1]
                    b = fill(s)[0]
                    wait_full(act, s, f)
                    wait_earlier(act, sum_ready, f, CHUNKS, c, first_f)
                    nc.scalar.activation(relu2, bank[b][:], ACT.Relu, bias=bi_sb[:, c:c + 1]).then_inc(taken[b], 1)
                elif kind == "split":
                    c = s[1]
                    act.wait_ge(sum_ready, f * CHUNKS + c + 1)
                    if c >= 2:
                        act.wait_ge(down_done, f * (CHUNKS - 1) + c - 1)
                    copy(h_hi[:, c % 2, :], relu_sum[:, c % 2, :]).then_inc(h_hi_ready, 1)

            def steps(todo, g, first=False, first_f=False):
                for s in todo:
                    step(s, g, g - 1, first, first_f)

            split_weights(first_weights, w_loaded)
            act.wait_ge(small_loaded, 16 * NSMALL)
            nc.scalar.activation(tanh_g[:], gates[:], ACT.Tanh).then_inc(tanh_ready, 1)
            split_context(0)
            steps(ATTENTION, 0, first=True)
            split_weights(late_weights, w2_loaded)
            steps(BOTH, 1, first_f=True)
            with act.Fori(2, GROUPS - 1) as g:
                steps(BOTH, g)
            steps(BOTH_LAST, GROUPS - 1)
            steps(LAST, GROUPS)

        @block.vector
        def _(dve):
            v = nc.vector
            chain_a = Chain(dve, dve_a, A_LINKS)
            chain_m = Chain(dve, dve_m, M_LINKS)

            def split_weights(weights, first):
                for n, (_, dst, stage) in enumerate(weights):
                    dve.wait_ge(w_hi, first + n + 1)
                    v.tensor_tensor(dst[1][:], stage, dst[0][:], ALU.subtract).then_inc(w_lo, 1)

            def layernorm(src, chain, ready):
                for t in range(TT):
                    last = v.bn_stats(stats[:, t, :], src[:, t, :])
                chain.link(last)
                hold(dve)
                for t in range(TT):
                    last = v.bn_aggr(moments[:, t, :], stats[:, t, :])
                chain.link(last)
                ve, y, w = nt[:, 0, :], nt[:, 1, :], nt[:, 2, :]
                chain.link(v.tensor_scalar(ve, moments[:, :, 1], EPS, None, ALU.add))
                chain.link(v.tensor_scalar(y.bitcast(I32), ve.bitcast(I32), 1, None, ALU.logical_shift_right))
                chain.link(v.tensor_scalar(y.bitcast(I32), y.bitcast(I32), -1.0, float(RSQRT_MAGIC), ALU.mult, ALU.add))
                for _ in range(NEWTON):
                    chain.link(v.tensor_tensor(w, y, y, ALU.mult))
                    chain.link(v.tensor_tensor(w, w, ve, ALU.mult))
                    chain.link(v.tensor_scalar(w, w, -0.5, 1.5, ALU.mult, ALU.add))
                    chain.link(v.tensor_tensor(y, y, w, ALU.mult))
                for t in range(TT):
                    last = v.tensor_scalar(xn[:, t, :], src[:, t, :], moments[:, t, 0:1], nt[:, 1, t:t + 1], ALU.subtract, ALU.mult)
                last.then_inc(ready, 1)

            def lo_part(s, g, hi_sem, hi_count, dst, hi):
                b = fill(s)[0]
                dve.wait_ge(hi_sem, hi_count)
                v.tensor_tensor(dst, bank[b][:], hi, ALU.subtract).then_inc(taken[b], 1)

            def wide(t2):
                return t2.unsqueeze(2).to_broadcast([P, TT, EXPERTS])

            def route():
                link = chain_m.link
                mx, sm, rs, m1, k1, m2, k2 = (tk[:, i, :] for i in range(7))
                link(v.tensor_reduce(mx, lg[:], AX.X, ALU.max))
                v.tensor_tensor(lg[:], lg[:], wide(mx), ALU.subtract).then_inc(logits_shifted, 1)
                dve.wait_ge(exp_ready, chain_m.group + 1)
                link(v.tensor_reduce(sm, pr[:], AX.X, ALU.add))
                link(v.reciprocal(rs, sm))
                link(v.tensor_tensor(pr[:], pr[:], wide(rs), ALU.mult))
                link(v.tensor_reduce(m1, pr[:], AX.X, ALU.max))
                for m, k, one, p in ((m1, k1, one1, pr), (m2, k2, one2, pr2)):
                    if p is pr2:
                        link(v.scalar_tensor_tensor(out=pr2[:].rearrange("p t e -> p (t e)"), in0=one1[:].rearrange("p t e -> p (t e)"),
                                                    scalar=-2.0, in1=pr[:].rearrange("p t e -> p (t e)"), op0=ALU.mult, op1=ALU.add))
                        link(v.tensor_reduce(m2, pr2[:], AX.X, ALU.max))
                    link(v.tensor_tensor(key[:], p[:], wide(m), ALU.is_ge))
                    link(v.tensor_tensor(key[:], key[:], rank_sb[:].unsqueeze(1).to_broadcast([P, TT, EXPERTS]), ALU.mult))
                    link(v.tensor_reduce(k, key[:], AX.X, ALU.max))
                    link(v.tensor_tensor(one[:], key[:], wide(k), ALU.is_equal))
                link(v.tensor_tensor(gate_val[:], m1, m2, ALU.add))
                v.tensor_scalar(gate_val[:], gate_val[:], tanh_g[:, 1:2], None, ALU.mult)
                link(v.tensor_tensor(one2[:], one2[:], one1[:], ALU.subtract))
                for one, dst in ((one1, a_first), (one2, a_diff)):
                    last = v.tensor_tensor(dst.rearrange("p t (e r) -> p (t e) r", e=EXPERTS),
                                           a_all.rearrange("p t (e r) -> p (t e) r", e=EXPERTS),
                                           one[:].rearrange("p t e -> p (t e)").unsqueeze(2).to_broadcast([P, TT * EXPERTS, RANK]), ALU.mult)
                last.then_inc(routed, 1)

            HI_A, HI_M = 8, 6

            def step(s, g, f, first, first_f):
                kind = s[0]
                if kind == "next ln1":
                    dve.wait_ge(x_loaded, 16 * (g + 2))
                    layernorm(xin, chain_a, xn1_ready)
                elif kind == "xT":
                    lo_part(s, g, hi_a, g * HI_A + 2 + s[1] + 1, xT_lo[:, s[1], :], xT_hi[:, s[1], :])
                elif kind == "q":
                    lo_part(s, g, hi_a, g * HI_A + 4 + s[1] + 1, q_lo[:, s[1], :], q_hi[:, s[1], :])
                elif kind == "k":
                    lo_part(s, g, hi_a, g * HI_A + s[1] + 1, k_lo[:, s[1], :], k_hi[:, s[1], :])
                elif kind == "S":
                    _, bt, quad, part = s
                    b = fill(s)[0]
                    wait_full(dve, s, g)
                    width = P if part == 0 else SEQ
                    h0 = 4 * quad + (0 if part == 0 else 2 * part - 2)
                    n = 512 // width
                    v.tensor_reduce(neg_max[:, bt, min(part, 1), h0:h0 + n], bank[b][:].rearrange("p (n w) -> p n w", w=width),
                                    AX.X, ALU.max, negate=True).then_inc(taken[b], 1)
                elif kind == "oT":
                    t = s[1]
                    b = fill(s)[0]
                    wait_full(dve, s, g)
                    heads = bank[b][:].rearrange("p (h c) -> p h c", h=HEADS)
                    chain_a.link(v.reciprocal(inv_sum[:, t], heads[:, :, HD]))
                    v.tensor_tensor(att[:, t], heads[:, :, 0:HD], inv_sum[:, t].unsqueeze(2).to_broadcast([P, HEADS, HD]),
                                    ALU.mult).then_inc(taken[b], 1)
                elif kind == "nT":
                    b = fill(s)[0]
                    dve.wait_ge(hi_a, g * HI_A + 6 + s[1] + 1)
                    where = (slice(None), slice(None), slice(s[1] * SEQ, (s[1] + 1) * SEQ))
                    v.tensor_tensor(att_lo[where], bank[b][:].rearrange("p (m t) -> p m t", m=DK), att_hi[where],
                                    ALU.subtract).then_inc(taken[b], 1)
                elif kind == "wo":
                    b = fill(s)[0]
                    wait_full(dve, s, f)
                    if s[1] == 0:
                        dve.wait_ge(res_loaded, 16 * (f + 1))
                    v.scalar_tensor_tensor(out=x1[:, 2 * s[1]:2 * s[1] + 2, :].rearrange("p t d -> p (t d)"), in0=bank[b][:],
                                           scalar=tanh_g[:, 0:1], in1=x1[:, 2 * s[1]:2 * s[1] + 2, :].rearrange("p t d -> p (t d)"),
                                           op0=ALU.mult, op1=ALU.add).then_inc(taken[b], 1)
                elif kind == "ln2":
                    wait_taken(dve, ("wo", 0), f)
                    wait_taken(dve, ("wo", 1), f)
                    layernorm(x1, chain_m, xn2_ready)
                elif kind == "x2T":
                    lo_part(s, f, hi_m, f * HI_M + s[1] + 1, xT_lo[:, s[1], :], xT_hi[:, s[1], :])
                elif kind == "ag":
                    b = fill(s)[0]
                    dve.wait_ge(hi_m, f * HI_M + 2 + s[1] + 1)
                    v.tensor_tensor(lg[:, 2 * s[1]:2 * s[1] + 2, :], bank[b][:].rearrange("p (t c) -> p t c", t=2)[:, :, P:NAG],
                                    gb_sb[:].unsqueeze(1).to_broadcast([P, 2, EXPERTS]), ALU.add).then_inc(taken[b], 1)
                elif kind == "route":
                    wait_taken(dve, ("ag", 0), f)
                    wait_taken(dve, ("ag", 1), f)
                    route()
                elif kind == "aT":
                    lo_part(s, f, hi_m, f * HI_M + 4 + s[1] + 1, (a1_lo, a2_lo)[s[1]][:, 0, :], (a1_hi, a2_hi)[s[1]][:, 0, :])
                elif kind == "up2":
                    c = s[1]
                    wait_taken(dve, s, f)
                    wait_earlier(dve, h_ready, f, CHUNKS, c - 1, first_f)
                    v.tensor_tensor(relu_sum[:, c % 2, :], relu1[:, c % 2, :], relu2, ALU.add).then_inc(sum_ready, 1)
                elif kind == "out":
                    p = s[1]
                    wait_full(dve, ("down", p), f)
                    if not first_f:
                        dve.wait_ge(out_stored, f * 32)
                    ins = v.tensor_tensor(fin[:, 2 * p:2 * p + 2, :], bank[6 + p][:].rearrange("p (t d) -> p t d", t=2),
                                          bo2[:].unsqueeze(1).to_broadcast([P, 2, D]), ALU.add)
                    ins.then_inc(taken[6 + p], 1)
                    wait_taken(dve, ("down", p), f)
                    for t in (2 * p, 2 * p + 1):
                        last = v.scalar_tensor_tensor(out=fin[:, t, :], in0=fin[:, t, :], scalar=gate_val[:, t:t + 1],
                                                      in1=x1[:, t, :], op0=ALU.mult, op1=ALU.add)
                    last.then_inc(out_ready, 1)

            def steps(todo, g, first=False, first_f=False):
                chain_a.start(g)
                chain_m.start(g - 1)
                for s in todo:
                    step(s, g, g - 1, first, first_f)
                assert chain_a.n in (0, A_LINKS, A_LINKS - LN_LINKS) and chain_m.n in (0, M_LINKS), (chain_a.n, chain_m.n)

            v.memset(v_ones[:], 1.0)
            for e in range(EXPERTS):
                v.memset(rank_sb[:, e:e + 1], float(EXPERTS - e))
            for half in (32, 96):
                last = v.memset(k_stack[half:half + 32, :, :].bitcast(F32), 1.0)
            last.then_inc(consts, 1)
            split_weights(first_weights, 0)
            dve.wait_ge(small_loaded, 16 * NSMALL)
            v.tensor_scalar(bo2[:], bo2[:], 2.0, None, ALU.mult).then_inc(dve_setup, 1)
            dve.wait_ge(dve_setup, 1)
            dve.wait_ge(tanh_ready, 1)
            chain_0 = Chain(dve, dve_0, 0)
            dve.wait_ge(x_loaded, 16)
            layernorm(xin, chain_0, xn1_ready)
            steps(ATTENTION, 0, first=True)
            split_weights(late_weights, NW)
            steps(BOTH, 1, first_f=True)
            with dve.Fori(2, GROUPS - 1) as g:
                steps(BOTH, g)
            steps(BOTH_LAST, GROUPS - 1)
            steps(LAST, GROUPS)

        @block.gpsimd
        def _(pool):
            p_ = nc.gpsimd

            def split_context(g):
                pool.wait_ge(c_hi_ready, g + 1)
                p_.tensor_tensor(c_lo[:], cin[:], c_hi[:], ALU.subtract).then_inc(c_lo_ready, 1)

            def step(s, g, f, first, first_f):
                kind = s[0]
                if kind == "next cx":
                    split_context(g + 1)
                elif kind == "ST":
                    _, b, quad, part = s
                    wait_taken(pool, s, g)
                    hold(pool)
                    n, width = (4, P) if part == 2 else (2, SEQ)
                    blk = probs[:, (b * QUADS + quad) % 2, part, :].rearrange("p (n w) -> p n w", n=n)[:, :, 0:P]
                    p_.affine_select(out=blk, in_=blk, pattern=[[0, n], [1, P]], compare_op=ALU.is_ge, fill=0.0,
                                     base=0, channel_multiplier=-1).then_inc(masked, 1)
                elif kind == "split":
                    c = s[1]
                    pool.wait_ge(h_hi_ready, f * CHUNKS + c + 1)
                    p_.tensor_tensor(h_lo[:, c % 2, :], relu_sum[:, c % 2, :], h_hi[:, c % 2, :], ALU.subtract).then_inc(h_ready, 1)

            def steps(todo, g, first=False, first_f=False):
                for s in todo:
                    step(s, g, g - 1, first, first_f)

            p_.memset(ident[:], 0.0)
            p_.memset(causal[:], 0.0).then_inc(pool_step, 1)
            pool.wait_ge(pool_step, 1)
            p_.affine_select(out=ident[:], in_=ident[:], pattern=[[-1, P]], compare_op=ALU.not_equal, fill=1.0,
                             base=0, channel_multiplier=1)
            p_.affine_select(out=causal[:], in_=causal[:], pattern=[[0, 4], [-1, P]], compare_op=ALU.is_ge, fill=MASKED,
                             base=0, channel_multiplier=1).then_inc(pool_step, 1)
            pool.wait_ge(pool_step, 2)
            p_.tensor_copy(ident_b[:], ident[:]).then_inc(consts, 1)
            split_context(0)
            steps(ATTENTION, 0, first=True)
            steps(BOTH, 1, first_f=True)
            with pool.Fori(2, GROUPS - 1) as g:
                steps(BOTH, g)
            steps(BOTH_LAST, GROUPS - 1)
            steps(LAST, GROUPS)


def kernel(x, ctx_1024, g_xattn, g_ffn, L0_xattn_wq, L0_xattn_wk, L0_xattn_wv, L0_xattn_wo, L0_ffn_wi, L0_ffn_bi,
           L0_ffn_wo, L0_ffn_bo, L0_ffn_lora_A, L0_ffn_lora_B, L0_ffn_gate_w, L0_ffn_gate_b):
    import concourse.bacc as bacc
    from concourse.bass_utils import run_bass_kernel_spmd

    def lay(a):
        return np.ascontiguousarray(a)

    x = np.asarray(x)
    arrays = {
        "x": lay(x.reshape(BATCH * SEQ, D)),
        "ctxT": lay(np.asarray(ctx_1024).reshape(BATCH * SEQ, D).T),
        "g_xattn": lay(g_xattn),
        "g_ffn": lay(g_ffn),
        "wqT": lay(np.asarray(L0_xattn_wq).T),
        "wkT": lay(np.asarray(L0_xattn_wk).T),
        "wvT": lay(np.asarray(L0_xattn_wv).T),
        "woT": lay(np.asarray(L0_xattn_wo).T),
        "wiT": lay(np.asarray(L0_ffn_wi).T),
        "bi": lay(np.asarray(L0_ffn_bi).reshape(CHUNKS, P).T),
        "w2T": lay(np.asarray(L0_ffn_wo).T),
        "bo": lay(L0_ffn_bo),
        "abT": lay(np.concatenate([np.asarray(L0_ffn_lora_A).reshape(EXPERTS * RANK, D), np.asarray(L0_ffn_gate_w)]).T),
        "bT": lay(np.asarray(L0_ffn_lora_B).transpose(0, 2, 1).reshape(EXPERTS * RANK, FF)),
        "gate_b": lay(L0_ffn_gate_b),
    }
    nc = bacc.Bacc("TRN2", target_bir_lowering=False, num_devices=1)
    args = [nc.dram_tensor(f"in_{n}", a.shape, mybir.dt.from_np(a.dtype), kind="ExternalInput").ap() for n, a in arrays.items()]
    out = nc.dram_tensor("out", (BATCH * SEQ, D), F32, kind="ExternalOutput").ap()
    flamingo_layer(nc, *args, out)
    r = run_bass_kernel_spmd(nc, [{f"in_{n}": a for n, a in arrays.items()}], core_ids=[0])
    return r.results[0]["out"].reshape(BATCH, SEQ, D)
```

```python
from contextlib import ExitStack

import numpy as np
import concourse.bass as bass
from concourse import mybir

F32 = mybir.dt.float32
F32R = mybir.dt.float32r
BF16 = mybir.dt.bfloat16
I32 = mybir.dt.int32
ALU = mybir.AluOpType
ACT = mybir.ActivationFunctionType
AX = mybir.AxisListType

P = 128
BATCH, SEQ, D = 16, 256, 256
HEADS, HD = 16, 16
FF, EXPERTS, RANK = 1024, 8, 16
EPS = 1e-5
GB = 2
GT = GB * SEQ
GROUPS = BATCH // GB
TT = GT // P
DK = D // P
QUADS = HEADS // 4
HSLOT = 32
CHUNKS = FF // P
NAG = EXPERTS * RANK + EXPERTS
SPLITS = 3
SROWS = SPLITS * HD
HALF = 8
SCALE = 1.0 / float(np.sqrt(HD))
MASKED = -1e30
RSQRT_MAGIC = 0x5F3759DF


def plan(fills):
    count, where = {}, {}
    for name, bank in fills:
        where[name] = (bank, count.get(bank, 0))
        count[bank] = count.get(bank, 0) + 1
    return where, count


HEAD = [("k", 0), ("k", 1), ("xT", 0), ("xT", 1), ("q", 0), ("q", 1)]
VALUES = [("v", 0), ("v", 1)]
SCORES = []
for _b in range(GB):
    SCORES += [("S", _b, _q, _p) for _q in range(QUADS) for _p in range(3)] + [("mT", _b)]
PROBS = []
for _u in range(GB * QUADS + 1):
    if _u < GB * QUADS:
        PROBS += [("ST", _u // QUADS, _u % QUADS, _p) for _p in range(3)]
    if _u > 0:
        _v = _u - 1
        PROBS += [("AV", _v // QUADS, _v % QUADS)]
        if _v % 2:
            PROBS += [("raw", _v // QUADS, (_v % QUADS) // 2)]
    if _u == QUADS + 1:
        PROBS += [("oT", 0), ("oT", 1)]
    if _u == QUADS + 2:
        PROBS += [("nT", 0)]
TAIL = [("oT", 2), ("oT", 3), ("nT", 1)]
FFN = []
for _c in range(CHUNKS + 3):
    if _c == 1:
        FFN.append(("aT", 1))
    if _c < CHUNKS:
        FFN.append(("up1", _c))
    if 0 <= _c - 1 < CHUNKS:
        FFN.append(("up2", _c - 1))
    if 0 <= _c - 2 < CHUNKS:
        FFN.append(("split", _c - 2))
    if 0 <= _c - 3 < CHUNKS:
        FFN.append(("down", _c - 3))
    if _c in (2, 3):
        FFN.append(("bias", _c - 2))
FFN += [("out", 0), ("out", 1)]
EARLY_UPS = (0, 1)
MID = [("wo", 0), ("wo", 1), ("ln2",), ("x2T", 0), ("x2T", 1), ("ag", 0), ("ag", 1), ("route",),
       ("wi", 0), ("wi", 1), ("aT", 0)]
M_FILLS, M_COUNT = plan([(("wo", 0), 4), (("wo", 1), 5), (("x2T", 0), 6), (("x2T", 1), 7), (("ag", 0), 4),
                         (("ag", 1), 5), (("aT", 0), 6), (("aT", 1), 7)]
                        + [f for c in range(CHUNKS) for f in ((("up1", c), 4 + c % 2), (("up2", c), 4 + c % 2))]
                        + [(("down", 0), 6), (("down", 1), 7)])


def merge(a, b):
    out, i, j = [], 0, 0
    while i < len(a) or j < len(b):
        if j >= len(b) or (i < len(a) and i * len(b) <= j * len(a)):
            out.append(a[i])
            i += 1
        else:
            out.append(b[j])
            j += 1
    return out


def after(steps, at, more):
    n = steps.index(at) + 1
    return steps[:n] + more + steps[n:]


START = HEAD
EARLY = 10
_first = SCORES[EARLY:SCORES.index(("mT", 0))]
_second = [s for s in SCORES if s[:2] == ("S", 1)]
_attention = (_first + _second[:1] + [("mT", 0)] + _second[1:3] + merge(_second[3:], PROBS[:7]) + [("mT", 1)]
              + PROBS[7:])
_middle = merge(_attention, FFN[:-4])
_middle = after(_middle, ("ST", 0, 3, 2), [("next ln1",)])
_middle = after(_middle, ("up1", CHUNKS - 1), HEAD[2:4])
_middle = after(_middle, ("ST", 1, 0, 2), HEAD[0:2])
_middle = after(_middle, ("ST", 1, 2, 1), HEAD[4:5])
_middle = after(_middle, ("AV", 1, 2), HEAD[5:6])
BOTH = ([("wo", 0), ("wo", 1)] + VALUES[:1] + [("ln2",)] + SCORES[:3] + [("x2T", 0), ("x2T", 1)] + SCORES[3:5]
        + [("ag", 0), ("ag", 1), ("route",)] + VALUES[1:] + SCORES[5:8] + [("wi", 0), ("wi", 1)] + SCORES[8:EARLY]
        + [("next cx",), ("aT", 0)] + _middle + TAIL[:2] + FFN[-4:-3] + TAIL[2:] + FFN[-3:])
M_STEPS = MID + FFN
BOTH_LAST = [s for s in BOTH if s not in HEAD and s[0][:4] != "next"]
ATTENTION = [s for s in BOTH if s not in M_STEPS]
ATTENTION_0 = ATTENTION
for _n in range(3):
    ATTENTION_0 = after(ATTENTION_0, ("ST", 0, _n, 2), [("late weight", _n)])
LAST = M_STEPS
NO_FILL = ("raw", "next ln1", "next cx")

PRE_FILLS, PRE_COUNT = plan([(s, n % 3) for n, s in enumerate(START)])
_fills, _n3, _n4 = [], 0, 0
for _s in ATTENTION:
    if _s[0] == "v" or _s[:2] == ("S", 0):
        _fills.append((_s, _n4 % 4))
        _n4 += 1
    elif _s[0] == "AV":
        if _s[2] % 2:
            _fills.append((("AV", _s[1], _s[2] // 2), 3))
    elif _s[0] not in NO_FILL:
        _fills.append((_s, _n3 % 3))
        _n3 += 1
A_FILLS, A_COUNT = plan(_fills)
LAST_A_FILLS, _ = plan([f for f in _fills if f[0] not in HEAD])
M_KINDS = {s[0] for s in MID + FFN}

NEWTON = 3
LN_LINKS = 5 + 3 * NEWTON
ROUTE_LINKS = 16
A_LINKS = LN_LINKS + TT
M_LINKS = LN_LINKS + ROUTE_LINKS
STACK_DMAS = 2 * DK


class Chain:

    def __init__(self, eng, sem, per):
        self.eng, self.sem, self.per, self.n, self.group = eng, sem, per, 0, 0

    def start(self, group):
        self.group, self.n = group, 0

    def link(self, ins):
        self.n += 1
        ins.then_inc(self.sem, 1)
        self.eng.wait_ge(self.sem, self.group * self.per + self.n)


def flamingo_layer(nc, x, ctxT, g_xattn, g_ffn, wqT, wkT, wvT, woT, wiT, bi, w2T, bo, abT, bT, gate_b, out):
    with ExitStack() as ctx:
        def sb(name, shape, dt):
            return ctx.enter_context(nc.sbuf_tensor(name, shape, dt))

        def sem(name):
            return ctx.enter_context(nc.semaphore(name))

        bank = [ctx.enter_context(nc.psum_tensor(f"bank{i}", [P, 512], F32)) for i in range(8)]

        def pair(name, n, cols):
            return sb(name + "_hi", [P, n, cols], F32R), sb(name + "_lo", [P, n, cols], F32R)

        wq, wk, wv = pair("wq", DK, D), pair("wk", DK, D), pair("wv", DK, D)
        wo = pair("wo", DK, D)
        ab_flat = sb("ab_flat", [P, 2 * DK * NAG + D - NAG], F32R)
        ab = [ab_flat[:, i * DK * NAG:(i + 1) * DK * NAG].rearrange("p (n c) -> p n c", n=DK) for i in range(2)]
        wb = pair("wb", 1, FF)
        wi = pair("wi", DK, FF)
        w2 = pair("w2", CHUNKS, D)
        bi_sb = sb("bi_sb", [P, CHUNKS], F32)
        bo2 = sb("bo2", [P, D], F32)
        gb_sb = sb("gb_sb", [P, EXPERTS], F32)
        rank_sb = sb("rank_sb", [P, EXPERTS], F32)
        gates = sb("gates", [P, 2], F32)
        tanh_g = sb("tanh_g", [P, 2], F32)
        ident = sb("ident", [P, P], F32)
        ident_b = sb("ident_b", [P, P], BF16)
        causal = sb("causal", [P, 1, P], BF16)

        xin = sb("xin", [P, TT, D], F32)
        cin = sb("cin", [P, DK, GT], F32)
        c_hi, c_lo = pair("c", DK, GT)
        xn = sb("xn", [P, TT, D], F32)
        xT_hi, xT_lo = pair("xT", DK, GT)
        scratch = sb("scratch", [P, 5120], F32)
        compact = scratch[:, 3072:5120].bitcast(F32R).rearrange("p (m s t) -> p m s t", m=DK, s=2)
        probs = scratch[:, 0:3072].rearrange("p (s a t) -> p s a t", s=2, a=3)
        q_stack = sb("q_stack", [P, HALF, GT], F32R)
        k_stack = sb("k_stack", [P, HALF, GT], F32R)
        v_ones = sb("v_ones", [P, TT, HEADS, HSLOT], F32)
        neg_max = sb("neg_max", [P, GB, 2, HEADS], F32)
        max_row = sb("max_row", [2 * HEADS, GB, P], F32R)
        inv_sum = sb("inv_sum", [P, TT, HEADS], F32)
        raw = sb("raw", [P, QUADS, GT], F32)
        att = sb("att", [P, TT, HEADS, HD], F32)
        att_hi, att_lo = pair("att", DK, GT)

        work = sb("work", [P, 5120], F32)
        x1 = work[:, 0:1024].rearrange("p (t d) -> p t d", t=TT)
        fin = work[:, 1024:2048].rearrange("p (t d) -> p t d", t=TT)
        a_all = work[:, 2048:2560].rearrange("p (t e) -> p t e", t=TT)
        a_first = work[:, 2560:3072].rearrange("p (t e) -> p t e", t=TT)
        a_diff = work[:, 3072:3584].rearrange("p (t e) -> p t e", t=TT)
        relu1 = work[:, 3584:4608].rearrange("p (s t) -> p s t", s=2)
        relu2 = work[:, 4608:5120]
        relu_sum = work[:, 2048:3072].rearrange("p (s t) -> p s t", s=2)
        a1_hi, a1_lo = pair("a1", 1, GT)
        a2_hi, a2_lo = pair("a2", 1, GT)
        h_hi, h_lo = pair("h", 2, GT)
        stats = sb("stats", [P, TT, 6], F32)
        moments = sb("moments", [P, TT, 2], F32)
        nt = sb("nt", [P, 3, TT], F32)
        lg = sb("lg", [P, TT, EXPERTS], F32)
        pr = sb("pr", [P, TT, EXPERTS], F32)
        pr2 = sb("pr2", [P, TT, EXPERTS], F32)
        key = sb("key", [P, TT, EXPERTS], F32)
        one1 = sb("one1", [P, TT, EXPERTS], F32)
        one2 = sb("one2", [P, TT, EXPERTS], F32)
        tk = sb("tk", [P, 8, TT], F32)
        gate_val = sb("gate_val", [P, TT], F32)

        full = [sem(f"full{i}") for i in range(8)]
        taken = [sem(f"taken{i}") for i in range(8)]
        w_loaded = [sem(f"w_loaded{i}") for i in range(8)]
        small_loaded = sem("small_loaded")
        w_hi = sem("w_hi")
        w_lo = sem("w_lo")
        consts = sem("consts")
        pool_step = sem("pool_step")
        tanh_ready = sem("tanh_ready")
        x_loaded = sem("x_loaded")
        c_loaded = sem("c_loaded")
        c_hi_ready = sem("c_hi_ready")
        c_lo_ready = sem("c_lo_ready")
        xn1_ready = sem("xn1_ready")
        res_loaded = sem("res_loaded")
        hi_h = sem("hi_h")
        hi_n = sem("hi_n")
        hi_m = sem("hi_m")
        q_stacked = sem("q_stacked")
        k_stacked = sem("k_stacked")
        k_spilled = [sem(f"k_spilled{m}") for m in range(DK)]
        q_spilled = [sem(f"q_spilled{m}") for m in range(DK)]
        max_stacked = [sem(f"max_stacked{b}") for b in range(GB)]
        masked = sem("masked")
        av_done = sem("av_done")
        xn2_ready = sem("xn2_ready")
        logits_shifted = sem("logits_shifted")
        exp_ready = sem("exp_ready")
        first_known = sem("first_known")
        first_masked = sem("first_masked")
        routed = sem("routed")
        biased = sem("biased")
        sum_ready = sem("sum_ready")
        h_hi_ready = sem("h_hi_ready")
        h_ready = sem("h_ready")
        down_done = sem("down_done")
        out_stored = sem("out_stored")
        dve_a = sem("dve_a")
        dve_m = sem("dve_m")
        dve_0 = sem("dve_0")
        dve_setup = sem("dve_setup")
        held = sem("held")

        def fill(step):
            where, count = (M_FILLS, M_COUNT) if step[0] in M_KINDS else (A_FILLS, A_COUNT)
            b, n = where[step]
            return b, n, count[b]

        def fills_until(step, g):
            if g is START:
                return PRE_FILLS[step][1] + 1
            b, n, per = fill(step)
            if isinstance(g, int) and g == GROUPS - 1 and step in LAST_A_FILLS:
                n = LAST_A_FILLS[step][1]
            return g * per + n + 1 + (0 if step[0] in M_KINDS else PRE_COUNT.get(b, 0))

        def bank_of(step, g):
            return PRE_FILLS[step][0] if g is START else fill(step)[0]

        def wait_full(eng, step, g):
            eng.wait_ge(full[bank_of(step, g)], fills_until(step, g))

        def wait_taken(eng, step, g):
            eng.wait_ge(taken[bank_of(step, g)], fills_until(step, g))

        def wait_free(eng, step, g, first):
            n = fills_until(step, g) - 1
            if not first or n > 0:
                eng.wait_ge(taken[bank_of(step, g)], n)

        def wait_earlier(eng, s, g, per, n, first):
            if not first or n > 0:
                eng.wait_ge(s, g * per + n)

        def masked_a(eng, dst, one):
            return eng.tensor_tensor(dst.rearrange("p t (e r) -> p (t e) r", e=EXPERTS),
                                     a_all.rearrange("p t (e r) -> p (t e) r", e=EXPERTS),
                                     one[:].rearrange("p t e -> p (t e)").unsqueeze(2).to_broadcast([P, TT * EXPERTS, RANK]),
                                     ALU.mult)

        def hold(eng):
            eng.sem_inc(held, 1)

        first_weights = []
        at = 0
        for dram, dst in ((wkT, wk), (wqT, wq), (wvT, wv), (woT, wo), (abT, ab)):
            n, cols = dst[0].shape[1], dst[0].shape[2]
            first_weights.append((dram.rearrange("(n p) c -> p n c", p=P), dst,
                                  scratch[:, at:at + n * cols].rearrange("p (n c) -> p n c", n=n)))
            at += n * cols
        late_weights = []
        at = 0
        for dram, dst in ((wiT, wi), (w2T, w2), (bT, wb)):
            n, cols = dst[0].shape[1], dst[0].shape[2]
            late_weights.append((dram.rearrange("(n p) c -> p n c", p=P), dst,
                                 work[:, at:at + n * cols].rearrange("p (n c) -> p n c", n=n)))
            at += n * cols
        NW = len(first_weights)
        HI_M = 6
        weights = first_weights + late_weights
        NSMALL = 5

        x_rows = x.rearrange("(g t p) d -> g p t d", p=P, t=TT)
        out_rows = out.rearrange("(g t p) d -> g p t d", p=P, t=TT)
        c_cols = ctxT.rearrange("(n p) (g t) -> g p n t", p=P, g=GROUPS)

        heads_dram = nc.dram_tensor("heads_dram", (2, DK, HALF, 2, HD, GT), F32, kind="Internal").ap()

        block = ctx.enter_context(nc.Block())

        @block.sync
        def _(sp):
            def load_group(g):
                sp.wait_ge(xn1_ready, g * TT)
                sp.wait_ge(c_lo_ready, g)
                hold(sp)
                sp.dma_start(xin[:], x_rows[g]).then_inc(x_loaded, 16)
                sp.dma_start(cin[:], c_cols[g]).then_inc(c_loaded, 16)

            def spill(kind, m, g):
                wait_taken(sp, (kind, m), g)
                for part in range(2):
                    sp.dma_start(heads_dram[int(kind == "k"), m, :, part],
                                 compact[:, m, part, :].bitcast(F32)).then_inc((q_spilled, k_spilled)[kind == "k"][m], 16)

            def stack(kind, g, dst, pair_at, single, single_at, s):
                for m in range(DK):
                    sp.wait_ge((q_spilled, k_spilled)[kind == "k"][m], (g + 1) * 32)
                    heads = heads_dram[int(kind == "k"), m].rearrange("h s d t -> (s d) h t")
                    for at_, part in ((pair_at, heads), (single_at, heads[HD * single:HD * (single + 1)])):
                        rows = 64 * m + at_
                        sp.dma_start(dst[rows:rows + part.shape[0], :, :].bitcast(F32), part).then_inc(s, 16)

            def stack_heads(g):
                stack("k", g, k_stack, 0, 0, 2 * HD, k_stacked)
                stack("q", g, q_stack, HD, 0, 0, q_stacked)

            def stack_max(g, b):
                wait_taken(sp, ("mT", b), g)
                for qt in range(2):
                    for m in range(DK):
                        row, head = 64 * m + SROWS, qt * HEADS + m * HALF
                        sp.dma_start(q_stack[row:row + 1, :, b * SEQ + qt * P:b * SEQ + (qt + 1) * P].bitcast(F32),
                                     max_row[head:head + HALF, b, :].bitcast(F32)).then_inc(max_stacked[b], 16)

            def store(f):
                for p in range(2):
                    wait_taken(sp, ("down", p), f)
                    hold(sp)
                    sp.dma_start(out_rows[f][:, 2 * p:2 * p + 2, :], fin[:, 2 * p:2 * p + 2, :]).then_inc(out_stored, 16)

            def load_residual(g, has_next):
                wait_full(sp, ("xT", 1), g) if has_next else wait_full(sp, ("x2T", 1), g - 1)
                hold(sp)
                sp.dma_start(xn[:], x_rows[g]).then_inc(res_loaded, 16)

            def group(g, first=False, load_next=True, has_next=True):
                for b in range(GB):
                    stack_max(g, b)
                if load_next:
                    load_group(g + 2)
                if has_next:
                    spill("k", 0, g)
                    spill("k", 1, g)
                load_residual(g, has_next)
                if has_next:
                    spill("q", 0, g)
                    spill("q", 1, g)
                    wait_full(sp, ("ST", GB - 1, QUADS - 1, 2), g)
                    hold(sp)
                    stack_heads(g + 1)
                if not first:
                    store(g - 1)

            def load_weight(n):
                src, _, stage = weights[n]
                sp.dma_start(stage, src).then_inc(w_loaded[n], 16)

            load_weight(0)
            sp.dma_start(cin[:], c_cols[0]).then_inc(c_loaded, 16)
            sp.dma_start(xin[:], x_rows[0]).then_inc(x_loaded, 16)
            for n in range(1, NW):
                load_weight(n)
            sp.dma_start(gates[:, 0:1], g_xattn.rearrange("(a b) -> a b", a=1).partition_broadcast(P)).then_inc(small_loaded, 16)
            sp.dma_start(gates[:, 1:2], g_ffn.rearrange("(a b) -> a b", a=1).partition_broadcast(P)).then_inc(small_loaded, 16)
            sp.dma_start(bi_sb[:], bi).then_inc(small_loaded, 16)
            sp.dma_start(bo2[:], bo.rearrange("(a b) -> a b", a=1).partition_broadcast(P)).then_inc(small_loaded, 16)
            sp.dma_start(gb_sb[:], gate_b.rearrange("(a b) -> a b", a=1).partition_broadcast(P)).then_inc(small_loaded, 16)
            sp.wait_ge(consts, 3)
            for kind, m in (("k", 0), ("k", 1), ("q", 0), ("q", 1)):
                spill(kind, m, START)
            stack_heads(0)
            load_group(1)
            for n in range(NW, len(weights)):
                load_weight(n)
            group(0, first=True)
            with sp.Fori(1, GROUPS - 2) as g:
                group(g)
            group(GROUPS - 2, load_next=False)
            group(GROUPS - 1, load_next=False, has_next=False)
            store(GROUPS - 1)
            sp.wait_ge(out_stored, 32 * GROUPS)

        @block.tensor
        def _(pe):
            def mm(*a, **k):
                return nc.tensor.matmul(*a, **k)

            def products(dst, lhs, rhs, tiles, more=False):
                todo = [(i, a, b) for i in range(tiles) for a, b in ((0, 0), (0, 1), (1, 0))]
                for n, (i, a, b) in enumerate(todo):
                    last = mm(dst, lhs[a](i), rhs[b](i), start=(n == 0 and not more), stop=(n == len(todo) - 1),
                              skip_group_check=more)
                return last

            def cols(pair_, lo, n):
                return [lambda i, t=t: t[:, i, lo:lo + n] for t in pair_]

            def step(s, g, f, first, first_f):
                kind = s[0]
                if kind in ("next cx", "next ln1", "ln2", "route", "bias", "split", "raw", "out"):
                    return
                if kind == "wi":
                    wait_free(pe, ("up1", s[1]), f, first_f)
                    products(bank[fill(("up1", s[1]))[0]][:], cols(wi, s[1] * P, P), cols((xT_hi, xT_lo), 0, GT), DK)
                    return
                if kind not in ("AV", "down"):
                    if not (kind == "up1" and s[1] in EARLY_UPS):
                        wait_free(pe, s, f if kind in M_KINDS else g, first_f if kind in M_KINDS else first)
                    ps = bank[bank_of(s, f if kind in M_KINDS else g)]
                of = 0 if g is START else g + 1
                if kind == "xT":
                    for t in range(TT):
                        if s[1] == 0:
                            pe.wait_ge(xn1_ready, of * TT + t + 1)
                        last = nc.tensor.transpose(ps[:, t * P:(t + 1) * P], xn[:, t, s[1] * P:(s[1] + 1) * P], ident[:])
                elif kind == "q":
                    if s[1] == 0:
                        wait_taken(pe, ("xT", 0), g)
                        wait_taken(pe, ("xT", 1), g)
                    last = products(ps[:], cols(wq, s[1] * P, P), cols((xT_hi, xT_lo), 0, GT), DK)
                elif kind == "k":
                    if s[1] == 0:
                        pe.wait_ge(c_hi_ready, of + 1)
                        pe.wait_ge(c_lo_ready, of + 1)
                    last = products(ps[:], cols(wk, s[1] * P, P), cols((c_hi, c_lo), 0, GT), DK)
                elif kind == "v":
                    for i in range(2):
                        last = products(ps[:, i * D:(i + 1) * D], cols((c_hi, c_lo), (2 * s[1] + i) * P, P), cols(wv, 0, D), DK)
                elif kind == "S":
                    _, b, quad, part = s
                    if (b, quad, part) == (0, 0, 0):
                        pe.wait_ge(q_stacked, (g + 1) * 16 * STACK_DMAS)
                        pe.wait_ge(k_stacked, (g + 1) * 16 * STACK_DMAS)
                    rows = slice(64 * (quad // 2), 64 * (quad // 2) + SROWS)
                    heads = range(4) if part == 0 else range(2 * part - 2, 2 * part)
                    width = P if part == 0 else SEQ
                    q0 = b * SEQ + (0 if part == 0 else P)
                    for n, j in enumerate(heads):
                        h = 4 * (quad % 2) + j
                        mm(ps[:, n * width:(n + 1) * width], q_stack[rows, h, q0:q0 + P],
                           k_stack[rows, h, b * SEQ:b * SEQ + width], start=(n == 0), stop=False, skip_group_check=True)
                    edge = ps[:].rearrange("p (n w) -> p n w", w=width)[:, :, width - P:width]
                    last = mm(edge, ident_b[:], causal[:].to_broadcast([P, len(heads), P]), start=False, stop=True, skip_group_check=True)
                elif kind == "mT":
                    wait_taken(pe, ("S", s[1], QUADS - 1, 2), g)
                    last = nc.tensor.transpose(ps[0:2 * HEADS, 0:P], neg_max[:, s[1]].rearrange("p a h -> p (a h)"), ident[:])
                elif kind == "ST":
                    _, b, quad, part = s
                    if (quad, part) == (0, 0):
                        pe.wait_ge(max_stacked[b], (g + 1) * 64)
                    rows = slice(64 * (quad // 2), 64 * (quad // 2) + SROWS + 1)
                    heads = range(4) if part == 2 else range(2 * part, 2 * part + 2)
                    width = P if part == 2 else SEQ
                    k0 = b * SEQ + (P if part == 2 else 0)
                    for n, j in enumerate(heads):
                        h = 4 * (quad % 2) + j
                        last = mm(ps[:, n * width:(n + 1) * width], k_stack[rows, h, k0:k0 + P],
                                  q_stack[rows, h, (b + 1) * SEQ - width:(b + 1) * SEQ], start=True, stop=True)
                elif kind == "AV":
                    _, b, quad = s
                    u = b * QUADS + quad
                    pe.wait_ge(masked, g * 3 * GB * QUADS + 3 * (u + 1))
                    ps = bank[3]
                    if quad % 2 == 0:
                        wait_free(pe, ("AV", b, quad // 2), g, first)
                    c0 = (quad % 2) * SEQ
                    for kt in range(2):
                        for j in range(4):
                            src = probs[:, u % 2, j // 2, (j % 2) * SEQ:(j % 2 + 1) * SEQ] if kt == 0 else \
                                probs[:, u % 2, 2, j * P:(j + 1) * P]
                            last = mm(ps[HSLOT * j:HSLOT * (j + 1), c0 + kt * P:c0 + SEQ],
                                      v_ones[:, 2 * b + kt, 4 * quad + j, :], src,
                                      start=(kt == 0), stop=(kt == 1), skip_group_check=True)
                    last.then_inc(full[3] if quad % 2 else av_done, 1)
                    return
                elif kind == "oT":
                    t = s[1]
                    wait_taken(pe, ("AV", t // 2, 1), g)
                    for quad in range(QUADS):
                        last = nc.tensor.transpose(ps[:, quad * P:(quad + 1) * P], raw[:, quad, t * P:(t + 1) * P], ident[:])
                elif kind == "nT":
                    b = s[1]
                    wait_taken(pe, ("oT", 2 * b + 1), g)
                    for m in range(DK):
                        for i in range(2):
                            last = nc.tensor.transpose(ps[:, m * SEQ + i * P:m * SEQ + (i + 1) * P],
                                                       att[:, 2 * b + i, m * HALF:(m + 1) * HALF, :].rearrange("p h d -> p (h d)"), ident[:])
                elif kind == "wo":
                    if s[1] == 0:
                        wait_taken(pe, ("nT", 0), f)
                        wait_taken(pe, ("nT", 1), f)
                    for i in range(2):
                        last = products(ps[:, i * D:(i + 1) * D], cols((att_hi, att_lo), (2 * s[1] + i) * P, P),
                                        cols(wo, 0, D), DK)
                elif kind == "x2T":
                    for t in range(TT):
                        if s[1] == 0:
                            pe.wait_ge(xn2_ready, f * TT + t + 1)
                        last = nc.tensor.transpose(ps[:, t * P:(t + 1) * P], xn[:, t, s[1] * P:(s[1] + 1) * P], ident[:])
                elif kind == "ag":
                    if s[1] == 0:
                        wait_taken(pe, ("x2T", 0), f)
                        wait_taken(pe, ("x2T", 1), f)
                    for i in range(2):
                        last = products(ps[:, i * D:(i + 1) * D], cols((xT_hi, xT_lo), (2 * s[1] + i) * P, P),
                                        [lambda j, part=part: ab_flat[:, (part * DK + j) * NAG:(part * DK + j) * NAG + D] for part in range(2)], DK)
                elif kind == "aT":
                    pe.wait_ge((first_masked, routed)[s[1]], f + 1)
                    src = (a_first, a_diff)[s[1]]
                    for t in range(TT):
                        last = nc.tensor.transpose(ps[:, t * P:(t + 1) * P], src[:, t, :], ident[:])
                elif kind == "up1":
                    c = s[1]
                    if c == 0:
                        wait_taken(pe, ("aT", 0), f)
                    if c not in EARLY_UPS:
                        products(ps[:], cols(wi, c * P, P), cols((xT_hi, xT_lo), 0, GT), DK)
                    last = products(ps[:], cols(wb, c * P, P), cols((a1_hi, a1_lo), 0, GT), 1, more=True)
                elif kind == "up2":
                    if s[1] == 0:
                        wait_taken(pe, ("aT", 1), f)
                    last = products(ps[:], cols(wb, s[1] * P, P), cols((a2_hi, a2_lo), 0, GT), 1, more=True)
                elif kind == "down":
                    c = s[1]
                    pe.wait_ge(h_ready, f * CHUNKS + c + 1)
                    for t in range(TT):
                        p = t // 2
                        if c == 0 and t % 2 == 0:
                            wait_free(pe, ("down", p), f, first_f)
                        dst = bank[6 + p][:, (t % 2) * D:(t % 2 + 1) * D]
                        for n, (a, b) in enumerate(((h_hi, 0), (h_hi, 1), (h_lo, 0))):
                            last = mm(dst, a[:, c % 2, t * P:(t + 1) * P], w2[b][:, c, :],
                                      start=(c == 0 and t % 2 == 0 and n == 0), stop=(c == CHUNKS - 1 and n == 2),
                                      skip_group_check=True)
                        if c == CHUNKS - 1 and t % 2:
                            last.then_inc(full[6 + p], 1)
                    if c < CHUNKS - 1:
                        last.then_inc(down_done, 1)
                    return
                last.then_inc(full[bank_of(s, f if kind in M_KINDS else g)], 1)

            def steps(todo, g, first=False, first_f=False):
                for s in todo:
                    step(s, g, None if g is START else g - 1, first, first_f)

            pe.wait_ge(consts, 1)
            pe.wait_ge(w_lo, 1)
            steps(START[:4], START, first=True)
            pe.wait_ge(w_lo, 2)
            steps(START[4:], START, first=True)
            pe.wait_ge(w_lo, NW)
            pe.wait_ge(consts, 4)
            steps(ATTENTION, 0, first=True)
            pe.wait_ge(w_lo, len(weights))
            steps(BOTH, 1, first_f=True)
            with pe.Fori(2, GROUPS - 1) as g:
                steps(BOTH, g)
            steps(BOTH_LAST, GROUPS - 1)
            steps(LAST, GROUPS)

        @block.scalar
        def _(act):
            def copy(dst, src):
                return nc.scalar.activation(dst, src, ACT.Copy)

            def split_weight(n):
                _, dst, stage = weights[n]
                act.wait_ge(w_loaded[n], 16)
                copy(dst[0][:], stage).then_inc(w_hi, 1)

            def split_context(g):
                act.wait_ge(c_loaded, 16 * (g + 1))
                copy(c_hi[:], cin[:]).then_inc(c_hi_ready, 1)

            def step(s, g, f, first, first_f):
                kind = s[0]
                if kind == "next cx":
                    split_context(g + 1)
                elif kind == "late weight":
                    split_weight(NW + s[1])
                elif kind == "xT":
                    wait_full(act, s, g)
                    copy(xT_hi[:, s[1], :], bank[bank_of(s, g)][:]).then_inc(hi_h, 1)
                elif kind in ("q", "k"):
                    wait_full(act, s, g)
                    of = 0 if g is START else g + 1
                    if kind == "q":
                        act.wait_ge(k_spilled[s[1]], (of + 1) * 32)
                    elif g is not START:
                        act.wait_ge(q_spilled[s[1]], of * 32)
                    copy(compact[:, s[1], 0, :], bank[bank_of(s, g)][:]).then_inc(hi_h, 1)
                elif kind == "v":
                    wait_full(act, s, g)
                    b = fill(s)[0]
                    for i in range(2):
                        last = copy(v_ones[:, 2 * s[1] + i, :, 0:HD], bank[b][:, i * D:(i + 1) * D].rearrange("p (h d) -> p h d", h=HEADS))
                    last.then_inc(taken[b], 1)
                elif kind == "mT":
                    wait_full(act, s, g)
                    b = fill(s)[0]
                    copy(max_row[:, s[1], :], bank[b][0:2 * HEADS, 0:P]).then_inc(taken[b], 1)
                elif kind == "ST":
                    _, bt, quad, part = s
                    u = bt * QUADS + quad
                    b = fill(s)[0]
                    wait_full(act, s, g)
                    if part == 0:
                        if quad % 2:
                            act.wait_ge(full[3], fills_until(("AV", bt, quad // 2), g) - 1)
                        else:
                            wait_earlier(act, av_done, g, GB * QUADS // 2, u // 2, first)
                    nc.scalar.activation(probs[:, u % 2, part, :], bank[b][:], ACT.Exp, scale=SCALE).then_inc(taken[b], 1)
                elif kind == "raw":
                    _, b, pair_ = s
                    wait_full(act, ("AV", b, pair_), g)
                    copy(raw[:, 2 * pair_:2 * pair_ + 2, b * SEQ:(b + 1) * SEQ],
                         bank[3][:].rearrange("p (q t) -> p q t", q=2)).then_inc(taken[3], 1)
                elif kind == "nT":
                    b = s[1]
                    wait_full(act, s, g)
                    copy(att_hi[:, :, b * SEQ:(b + 1) * SEQ],
                         bank[fill(s)[0]][:].rearrange("p (m t) -> p m t", m=DK)).then_inc(hi_n, 1)
                elif kind == "x2T":
                    wait_full(act, s, f)
                    copy(xT_hi[:, s[1], :], bank[fill(s)[0]][:]).then_inc(hi_m, 1)
                elif kind == "ag":
                    wait_full(act, s, f)
                    copy(a_all[:, 2 * s[1]:2 * s[1] + 2, :],
                         bank[fill(s)[0]][:].rearrange("p (t c) -> p t c", t=2)[:, :, 0:P]).then_inc(hi_m, 1)
                elif kind == "route":
                    act.wait_ge(logits_shifted, f + 1)
                    nc.scalar.activation(pr[:], lg[:], ACT.Exp).then_inc(exp_ready, 1)
                elif kind == "aT":
                    wait_full(act, s, f)
                    copy((a1_hi, a2_hi)[s[1]][:, 0, :], bank[fill(s)[0]][:]).then_inc(hi_m, 1)
                elif kind == "up1":
                    c = s[1]
                    b = fill(s)[0]
                    wait_full(act, s, f)
                    wait_earlier(act, sum_ready, f, CHUNKS, c - 1, first_f)
                    nc.scalar.activation(relu1[:, c % 2, :], bank[b][:], ACT.Relu, bias=bi_sb[:, c:c + 1]).then_inc(taken[b], 1)
                elif kind == "up2":
                    c = s[1]
                    b = fill(s)[0]
                    wait_full(act, s, f)
                    wait_earlier(act, sum_ready, f, CHUNKS, c, first_f)
                    nc.scalar.activation(relu2, bank[b][:], ACT.Relu, bias=bi_sb[:, c:c + 1]).then_inc(taken[b], 1)
                elif kind == "split":
                    c = s[1]
                    act.wait_ge(sum_ready, f * CHUNKS + c + 1)
                    if c >= 2:
                        act.wait_ge(down_done, f * (CHUNKS - 1) + c - 1)
                    copy(h_hi[:, c % 2, :], relu_sum[:, c % 2, :]).then_inc(h_hi_ready, 1)

            def steps(todo, g, first=False, first_f=False):
                for s in todo:
                    step(s, g, None if g is START else g - 1, first, first_f)

            split_weight(0)
            split_context(0)
            split_weight(1)
            steps(START, START, first=True)
            for n in range(2, NW):
                split_weight(n)
            act.wait_ge(small_loaded, 16 * NSMALL)
            nc.scalar.activation(tanh_g[:], gates[:], ACT.Tanh).then_inc(tanh_ready, 1)
            steps(ATTENTION_0, 0, first=True)
            steps(BOTH, 1, first_f=True)
            with act.Fori(2, GROUPS - 1) as g:
                steps(BOTH, g)
            steps(BOTH_LAST, GROUPS - 1)
            steps(LAST, GROUPS)

        @block.vector
        def _(dve):
            v = nc.vector
            chain_a = Chain(dve, dve_a, A_LINKS)
            chain_m = Chain(dve, dve_m, M_LINKS)

            def split_weight(n):
                _, dst, stage = weights[n]
                dve.wait_ge(w_hi, n + 1)
                v.tensor_tensor(dst[1][:], stage, dst[0][:], ALU.subtract).then_inc(w_lo, 1)

            def statistics(src, tiles, chain, more=False):
                for t in tiles:
                    last = v.bn_stats(stats[:, t, :], src[:, t, :])
                if not more:
                    chain.link(last)
                    hold(dve)

            def layernorm(src, chain, ready):
                for t in range(TT):
                    last = v.bn_aggr(moments[:, t, :], stats[:, t, :])
                chain.link(last)
                ve, y, w = nt[:, 0, :], nt[:, 1, :], nt[:, 2, :]
                chain.link(v.tensor_scalar(ve, moments[:, :, 1], EPS, None, ALU.add))
                chain.link(v.tensor_scalar(y.bitcast(I32), ve.bitcast(I32), 1, None, ALU.logical_shift_right))
                chain.link(v.tensor_scalar(y.bitcast(I32), y.bitcast(I32), -1.0, float(RSQRT_MAGIC), ALU.mult, ALU.add))
                for _ in range(NEWTON):
                    chain.link(v.tensor_tensor(w, y, y, ALU.mult))
                    chain.link(v.scalar_tensor_tensor(out=w, in0=w, scalar=-0.5, in1=ve, op0=ALU.mult, op1=ALU.mult))
                    chain.link(v.scalar_tensor_tensor(out=y, in0=w, scalar=1.5, in1=y, op0=ALU.add, op1=ALU.mult))
                for t in range(TT):
                    v.tensor_scalar(xn[:, t, :], src[:, t, :], moments[:, t, 0:1], nt[:, 1, t:t + 1], ALU.subtract,
                                    ALU.mult).then_inc(ready, 1)

            def lo_part(s, g, hi_sem, hi_count, dst, hi):
                b = fill(s)[0]
                dve.wait_ge(hi_sem, hi_count)
                v.tensor_tensor(dst, bank[b][:], hi, ALU.subtract).then_inc(taken[b], 1)

            def wide(t2):
                return t2.unsqueeze(2).to_broadcast([P, TT, EXPERTS])

            def route():
                link = chain_m.link
                mx, sm, rs, m1, k1, m2, k2 = (tk[:, i, :] for i in range(7))
                link(v.tensor_reduce(mx, lg[:], AX.X, ALU.max))
                v.tensor_tensor(lg[:], lg[:], wide(mx), ALU.subtract).then_inc(logits_shifted, 1)
                dve.wait_ge(exp_ready, chain_m.group + 1)
                link(v.tensor_reduce(sm, pr[:], AX.X, ALU.add))
                link(v.reciprocal(rs, sm))
                link(v.tensor_tensor(pr[:], pr[:], wide(rs), ALU.mult))
                link(v.tensor_reduce(m1, pr[:], AX.X, ALU.max))
                for m, k, one, p in ((m1, k1, one1, pr), (m2, k2, one2, pr2)):
                    if p is pr2:
                        link(v.scalar_tensor_tensor(out=pr2[:].rearrange("p t e -> p (t e)"), in0=one1[:].rearrange("p t e -> p (t e)"),
                                                    scalar=-2.0, in1=pr[:].rearrange("p t e -> p (t e)"), op0=ALU.mult, op1=ALU.add))
                        link(v.tensor_reduce(m2, pr2[:], AX.X, ALU.max))
                    link(v.tensor_tensor(key[:], p[:], wide(m), ALU.is_ge))
                    link(v.tensor_tensor(key[:], key[:], rank_sb[:].unsqueeze(1).to_broadcast([P, TT, EXPERTS]), ALU.mult))
                    link(v.tensor_reduce(k, key[:], AX.X, ALU.max))
                    ins = v.tensor_tensor(one[:], key[:], wide(k), ALU.is_equal)
                    if p is pr:
                        ins.then_inc(first_known, 1)
                        dve.wait_ge(first_known, chain_m.group + 1)
                    else:
                        link(ins)
                link(v.tensor_tensor(gate_val[:], m1, m2, ALU.add))
                v.tensor_scalar(gate_val[:], gate_val[:], tanh_g[:, 1:2], None, ALU.mult)
                link(v.tensor_tensor(one2[:], one2[:], one1[:], ALU.subtract))
                masked_a(v, a_diff, one2).then_inc(routed, 1)

            def step(s, g, f, first, first_f):
                kind = s[0]
                if kind == "late weight":
                    split_weight(NW + s[1])
                elif kind == "next ln1":
                    dve.wait_ge(x_loaded, 16 * (g + 2))
                    statistics(xin, range(TT), chain_a)
                    layernorm(xin, chain_a, xn1_ready)
                elif s in HEAD:
                    of = 0 if g is START else g + 1
                    order = HEAD if g is START else [x for x in BOTH if x in HEAD]
                    b = bank_of(s, g)
                    dve.wait_ge(hi_h, of * len(HEAD) + order.index(s) + 1)
                    if kind == "xT":
                        dst, hi = xT_lo[:, s[1], :], xT_hi[:, s[1], :]
                    else:
                        dst, hi = compact[:, s[1], 1, :], compact[:, s[1], 0, :]
                    v.tensor_tensor(dst, bank[b][:], hi, ALU.subtract).then_inc(taken[b], 1)
                elif kind == "S":
                    _, bt, quad, part = s
                    b = fill(s)[0]
                    wait_full(dve, s, g)
                    width = P if part == 0 else SEQ
                    h0 = 4 * quad + (0 if part == 0 else 2 * part - 2)
                    n = 512 // width
                    v.tensor_reduce(neg_max[:, bt, min(part, 1), h0:h0 + n], bank[b][:].rearrange("p (n w) -> p n w", w=width),
                                    AX.X, ALU.max, negate=True).then_inc(taken[b], 1)
                elif kind == "oT":
                    t = s[1]
                    b = fill(s)[0]
                    wait_full(dve, s, g)
                    heads = bank[b][:].rearrange("p (h c) -> p h c", h=HEADS)
                    chain_a.link(v.reciprocal(inv_sum[:, t], heads[:, :, HD]))
                    v.tensor_tensor(att[:, t], heads[:, :, 0:HD], inv_sum[:, t].unsqueeze(2).to_broadcast([P, HEADS, HD]),
                                    ALU.mult).then_inc(taken[b], 1)
                elif kind == "nT":
                    b = fill(s)[0]
                    dve.wait_ge(hi_n, g * GB + s[1] + 1)
                    where = (slice(None), slice(None), slice(s[1] * SEQ, (s[1] + 1) * SEQ))
                    v.tensor_tensor(att_lo[where], bank[b][:].rearrange("p (m t) -> p m t", m=DK), att_hi[where],
                                    ALU.subtract).then_inc(taken[b], 1)
                elif kind == "wo":
                    b = fill(s)[0]
                    wait_full(dve, s, f)
                    if s[1] == 0:
                        dve.wait_ge(res_loaded, 16 * (f + 1))
                        if first_f:
                            dve.wait_ge(w_lo, len(weights))
                        else:
                            hold(dve)
                            wait_taken(dve, ("down", 1), f - 1)
                    v.scalar_tensor_tensor(out=x1[:, 2 * s[1]:2 * s[1] + 2, :].rearrange("p t d -> p (t d)"), in0=bank[b][:],
                                           scalar=tanh_g[:, 0:1], in1=xn[:, 2 * s[1]:2 * s[1] + 2, :].rearrange("p t d -> p (t d)"),
                                           op0=ALU.mult, op1=ALU.add).then_inc(taken[b], 1)
                    wait_taken(dve, s, f)
                    hold(dve)
                    statistics(x1, (2 * s[1], 2 * s[1] + 1), chain_m, more=s[1] == 0)
                elif kind == "ln2":
                    layernorm(x1, chain_m, xn2_ready)
                elif kind == "x2T":
                    lo_part(s, f, hi_m, f * HI_M + s[1] + 1, xT_lo[:, s[1], :], xT_hi[:, s[1], :])
                elif kind == "ag":
                    b = fill(s)[0]
                    dve.wait_ge(hi_m, f * HI_M + 2 + s[1] + 1)
                    v.tensor_tensor(lg[:, 2 * s[1]:2 * s[1] + 2, :], bank[b][:].rearrange("p (t c) -> p t c", t=2)[:, :, P:NAG],
                                    gb_sb[:].unsqueeze(1).to_broadcast([P, 2, EXPERTS]), ALU.add).then_inc(taken[b], 1)
                elif kind == "route":
                    wait_taken(dve, ("ag", 0), f)
                    wait_taken(dve, ("ag", 1), f)
                    route()
                elif kind == "aT":
                    lo_part(s, f, hi_m, f * HI_M + 4 + s[1] + 1, (a1_lo, a2_lo)[s[1]][:, 0, :], (a1_hi, a2_hi)[s[1]][:, 0, :])
                elif kind == "bias":
                    if s[1] == 0:
                        dve.wait_ge(routed, f + 1)
                    for t in (2 * s[1], 2 * s[1] + 1):
                        last = v.scalar_tensor_tensor(out=x1[:, t, :], in0=bo2[:], scalar=gate_val[:, t:t + 1],
                                                      in1=x1[:, t, :], op0=ALU.mult, op1=ALU.add)
                    last.then_inc(biased, 1)
                elif kind == "up2":
                    c = s[1]
                    wait_taken(dve, s, f)
                    wait_earlier(dve, h_ready, f, CHUNKS, c - 1, first_f)
                    v.tensor_tensor(relu_sum[:, c % 2, :], relu1[:, c % 2, :], relu2, ALU.add).then_inc(sum_ready, 1)
                elif kind == "out":
                    p = s[1]
                    wait_full(dve, ("down", p), f)
                    dve.wait_ge(biased, f * 2 + p + 1)
                    if not first_f:
                        dve.wait_ge(out_stored, f * 32)
                    for i in range(2):
                        t = 2 * p + i
                        last = v.scalar_tensor_tensor(out=fin[:, t, :], in0=bank[6 + p][:, i * D:(i + 1) * D],
                                                      scalar=gate_val[:, t:t + 1], in1=x1[:, t, :], op0=ALU.mult, op1=ALU.add)
                    last.then_inc(taken[6 + p], 1)

            def steps(todo, g, first=False, first_f=False):
                if g is not START:
                    chain_a.start(g)
                    chain_m.start(g - 1)
                for s in todo:
                    step(s, g, None if g is START else g - 1, first, first_f)
                assert chain_a.n in (0, A_LINKS, A_LINKS - LN_LINKS) and chain_m.n in (0, M_LINKS), (chain_a.n, chain_m.n)

            split_weight(0)
            chain_0 = Chain(dve, dve_0, 0)
            dve.wait_ge(x_loaded, 16)
            statistics(xin, range(TT), chain_0)
            layernorm(xin, chain_0, xn1_ready)
            split_weight(1)
            steps(START, START, first=True)
            for e in range(EXPERTS):
                v.memset(rank_sb[:, e:e + 1], float(EXPERTS - e))
            for n in range(2, NW):
                split_weight(n)
            dve.wait_ge(small_loaded, 16 * NSMALL)
            v.tensor_scalar(bo2[:], bo2[:], 2.0, None, ALU.mult).then_inc(dve_setup, 1)
            dve.wait_ge(dve_setup, 1)
            dve.wait_ge(tanh_ready, 1)
            steps(ATTENTION_0, 0, first=True)
            steps(BOTH, 1, first_f=True)
            with dve.Fori(2, GROUPS - 1) as g:
                steps(BOTH, g)
            steps(BOTH_LAST, GROUPS - 1)
            steps(LAST, GROUPS)

        @block.gpsimd
        def _(pool):
            p_ = nc.gpsimd

            def split_context(g):
                pool.wait_ge(c_hi_ready, g + 1)
                p_.tensor_tensor(c_lo[:], cin[:], c_hi[:], ALU.subtract).then_inc(c_lo_ready, 1)

            def step(s, g, f, first, first_f):
                kind = s[0]
                if kind == "next cx":
                    split_context(g + 1)
                elif kind == "ST":
                    _, b, quad, part = s
                    wait_taken(pool, s, g)
                    hold(pool)
                    n, width = (4, P) if part == 2 else (2, SEQ)
                    blk = probs[:, (b * QUADS + quad) % 2, part, :].rearrange("p (n w) -> p n w", n=n)[:, :, 0:P]
                    p_.affine_select(out=blk, in_=blk, pattern=[[0, n], [1, P]], compare_op=ALU.is_ge, fill=0.0,
                                     base=0, channel_multiplier=-1).then_inc(masked, 1)
                elif kind == "route":
                    pool.wait_ge(first_known, f + 1)
                    hold(pool)
                    pool.wait_ge(hi_m, f * HI_M + 4)
                    masked_a(p_, a_first, one1).then_inc(first_masked, 1)
                elif kind == "split":
                    c = s[1]
                    pool.wait_ge(h_hi_ready, f * CHUNKS + c + 1)
                    p_.tensor_tensor(h_lo[:, c % 2, :], relu_sum[:, c % 2, :], h_hi[:, c % 2, :], ALU.subtract).then_inc(h_ready, 1)

            def steps(todo, g, first=False, first_f=False):
                for s in todo:
                    step(s, g, None if g is START else g - 1, first, first_f)

            p_.memset(ident[:], 0.0)
            p_.memset(causal[:], 0.0).then_inc(pool_step, 1)
            pool.wait_ge(pool_step, 1)
            p_.affine_select(out=ident[:], in_=ident[:], pattern=[[-1, P]], compare_op=ALU.not_equal, fill=1.0,
                             base=0, channel_multiplier=1)
            p_.affine_select(out=causal[:, 0, :], in_=causal[:, 0, :], pattern=[[-1, P]], compare_op=ALU.is_ge, fill=MASKED,
                             base=0, channel_multiplier=1).then_inc(pool_step, 1)
            pool.wait_ge(pool_step, 2)
            p_.tensor_copy(ident_b[:], ident[:]).then_inc(consts, 1)
            split_context(0)
            pool.wait_ge(c_lo_ready, 1)
            for n, half in enumerate((32, 96)):
                p_.memset(k_stack[half:half + 32, :, :].bitcast(F32), 1.0).then_inc(consts, 1)
                pool.wait_ge(consts, n + 2)
            p_.memset(v_ones[:], 1.0)
            p_.memset(ab_flat[:, 2 * DK * NAG:].bitcast(F32), 0.0).then_inc(consts, 1)
            steps(ATTENTION, 0, first=True)
            steps(BOTH, 1, first_f=True)
            with pool.Fori(2, GROUPS - 1) as g:
                steps(BOTH, g)
            steps(BOTH_LAST, GROUPS - 1)
            steps(LAST, GROUPS)


def kernel(x, ctx_1024, g_xattn, g_ffn, L0_xattn_wq, L0_xattn_wk, L0_xattn_wv, L0_xattn_wo, L0_ffn_wi, L0_ffn_bi,
           L0_ffn_wo, L0_ffn_bo, L0_ffn_lora_A, L0_ffn_lora_B, L0_ffn_gate_w, L0_ffn_gate_b):
    import concourse.bacc as bacc
    from concourse.bass_utils import run_bass_kernel_spmd

    def lay(a):
        return np.ascontiguousarray(a)

    x = np.asarray(x)
    arrays = {
        "x": lay(x.reshape(BATCH * SEQ, D)),
        "ctxT": lay(np.asarray(ctx_1024).reshape(BATCH * SEQ, D).T),
        "g_xattn": lay(g_xattn),
        "g_ffn": lay(g_ffn),
        "wqT": lay(np.asarray(L0_xattn_wq).T),
        "wkT": lay(np.asarray(L0_xattn_wk).T),
        "wvT": lay(np.asarray(L0_xattn_wv).T),
        "woT": lay(np.asarray(L0_xattn_wo).T),
        "wiT": lay(np.asarray(L0_ffn_wi).T),
        "bi": lay(np.asarray(L0_ffn_bi).reshape(CHUNKS, P).T),
        "w2T": lay(np.asarray(L0_ffn_wo).T),
        "bo": lay(L0_ffn_bo),
        "abT": lay(np.concatenate([np.asarray(L0_ffn_lora_A).reshape(EXPERTS * RANK, D), np.asarray(L0_ffn_gate_w)]).T),
        "bT": lay(np.asarray(L0_ffn_lora_B).transpose(0, 2, 1).reshape(EXPERTS * RANK, FF)),
        "gate_b": lay(L0_ffn_gate_b),
    }
    nc = bacc.Bacc("TRN2", target_bir_lowering=False, num_devices=1)
    args = [nc.dram_tensor(f"in_{n}", a.shape, mybir.dt.from_np(a.dtype), kind="ExternalInput").ap() for n, a in arrays.items()]
    out = nc.dram_tensor("out", (BATCH * SEQ, D), F32, kind="ExternalOutput").ap()
    flamingo_layer(nc, *args, out)
    r = run_bass_kernel_spmd(nc, [{f"in_{n}": a for n, a in arrays.items()}], core_ids=[0])
    return r.results[0]["out"].reshape(BATCH, SEQ, D)
```
